# Optimizing a Trainium2 kernel written in Bass

```python
import numpy as np
import jax
import jax.numpy as jnp

def _softmax(x, axis=-1):
    return jax.nn.softmax(x, axis=axis)

def _gelu(x):
    return jax.nn.gelu(x, approximate=True)

def _silu(x):
    return jax.nn.silu(x)

def _sigmoid(x):
    return jax.nn.sigmoid(x)

def _layernorm(x, axis=-1, eps=1e-05):
    m = jnp.mean(x, axis=axis, keepdims=True)
    v = jnp.var(x, axis=axis, keepdims=True)
    return (x - m) / jnp.sqrt(v + eps)

def _scatter_add(tgt, idx, src, axis=0):
    return tgt.at[idx].add(src)

def _segment_sum(src, seg, n):
    return jax.ops.segment_sum(src, seg, n)
kernel_name = 'mk_rec_standalone_d1_rec_r8_6b3016'

def setup_inputs(seed: int=0):
    np.random.seed(seed)
    _w = jnp.asarray

    def _rec_inputs():
        import jax
        import jax.numpy as jnp
        _rk = jax.random.key(seed)
        r_x = -0.000296005 + 1.00001 * jax.random.normal(jax.random.fold_in(_rk, 1), (512, 40, 64), jnp.float32)
        return r_x
    r_x = _rec_inputs()

    def _L0_rec_setup():
        import jax, jax.numpy as jnp
        import numpy as np
        B, F, E = (1024, 40, 64)
        NUM_UNITS = [64, 64, 64]
        NUM_HEADS = [2, 2, 2]
        LN_EPS = 1e-05

        def _mha(x, Wq, Wk, Wv, Wr, lnw, lnb, H, no):
            Bx, Fx, _ = x.shape

            def heads(W):
                return jnp.einsum('bfi,oi->bfo', x, W).reshape(Bx, Fx, H, no).transpose(0, 2, 1, 3)
            q, k, v = (heads(Wq), heads(Wk), heads(Wv))
            att = jax.nn.softmax(jnp.einsum('bhfd,bhgd->bhfg', q, k) / np.sqrt(no), axis=-1)
            o = jnp.einsum('bhfg,bhgd->bhfd', att, v)
            o = o.transpose(0, 2, 1, 3).reshape(Bx, Fx, H * no)
            o = jax.nn.relu(o + jnp.einsum('bfi,oi->bfo', x, Wr))
            mu = jnp.mean(o, axis=-1, keepdims=True)
            var = jnp.mean((o - mu) ** 2, axis=-1, keepdims=True)
            return (o - mu) * jax.lax.rsqrt(var + LN_EPS) * lnw + lnb
        key = jax.random.key(seed)
        ks = iter(jax.random.split(key, 32))
        inp = {'x': jax.random.normal(next(ks), (B, F, E), dtype=jnp.float32)}
        d_in = E
        for l, (nu, nh) in enumerate(zip(NUM_UNITS, NUM_HEADS)):
            d_out = nu * nh
            s = 1.0 / np.sqrt(d_in)
            for name in ['Wq', 'Wk', 'Wv', 'Wr']:
                inp[f'{name}{l}'] = jax.random.uniform(next(ks), (d_out, d_in), minval=-s, maxval=s, dtype=jnp.float32)
            inp[f'lnw{l}'] = jnp.ones((d_out,), jnp.float32)
            inp[f'lnb{l}'] = jnp.zeros((d_out,), jnp.float32)
            d_in = d_out
        inp['Wf'] = jax.random.normal(next(ks), (1, F * d_in), dtype=jnp.float32) * 0.01
        inp['bf'] = jnp.zeros((1,), jnp.float32)
        return inp
    _L0_rec_all = _L0_rec_setup()
    _L0_rec_in = {k: v for k, v in _L0_rec_all.items() if k in ('Wq0', 'Wk0', 'Wv0', 'Wr0', 'lnw0', 'lnb0', 'Wq1', 'Wk1', 'Wv1', 'Wr1', 'lnw1', 'lnb1', 'Wq2', 'Wk2', 'Wv2', 'Wr2', 'lnw2', 'lnb2', 'Wf', 'bf')}
    del _L0_rec_all
    return {'r_x': r_x, 'L0_rec_Wq0': _L0_rec_in['Wq0'], 'L0_rec_Wk0': _L0_rec_in['Wk0'], 'L0_rec_Wv0': _L0_rec_in['Wv0'], 'L0_rec_Wr0': _L0_rec_in['Wr0'], 'L0_rec_lnw0': _L0_rec_in['lnw0'], 'L0_rec_lnb0': _L0_rec_in['lnb0'], 'L0_rec_Wq1': _L0_rec_in['Wq1'], 'L0_rec_Wk1': _L0_rec_in['Wk1'], 'L0_rec_Wv1': _L0_rec_in['Wv1'], 'L0_rec_Wr1': _L0_rec_in['Wr1'], 'L0_rec_lnw1': _L0_rec_in['lnw1'], 'L0_rec_lnb1': _L0_rec_in['lnb1'], 'L0_rec_Wq2': _L0_rec_in['Wq2'], 'L0_rec_Wk2': _L0_rec_in['Wk2'], 'L0_rec_Wv2': _L0_rec_in['Wv2'], 'L0_rec_Wr2': _L0_rec_in['Wr2'], 'L0_rec_lnw2': _L0_rec_in['lnw2'], 'L0_rec_lnb2': _L0_rec_in['lnb2'], 'L0_rec_Wf': _L0_rec_in['Wf'], 'L0_rec_bf': _L0_rec_in['bf']}

def reference(r_x, L0_rec_Wq0, L0_rec_Wk0, L0_rec_Wv0, L0_rec_Wr0, L0_rec_lnw0, L0_rec_lnb0, L0_rec_Wq1, L0_rec_Wk1, L0_rec_Wv1, L0_rec_Wr1, L0_rec_lnw1, L0_rec_lnb1, L0_rec_Wq2, L0_rec_Wk2, L0_rec_Wv2, L0_rec_Wr2, L0_rec_lnw2, L0_rec_lnb2, L0_rec_Wf, L0_rec_bf):
    import jax
    import jax.numpy as jnp

    def _L0_rec_ref(x, Wq0, Wk0, Wv0, Wr0, lnw0, lnb0, Wq1, Wk1, Wv1, Wr1, lnw1, lnb1, Wq2, Wk2, Wv2, Wr2, lnw2, lnb2, Wf, bf):
        import jax, jax.numpy as jnp
        import numpy as np
        B, F, E = (1024, 40, 64)
        NUM_UNITS = [64, 64, 64]
        NUM_HEADS = [2, 2, 2]
        LN_EPS = 1e-05

        def _mha(x, Wq, Wk, Wv, Wr, lnw, lnb, H, no):
            Bx, Fx, _ = x.shape

            def heads(W):
                return jnp.einsum('bfi,oi->bfo', x, W).reshape(Bx, Fx, H, no).transpose(0, 2, 1, 3)
            q, k, v = (heads(Wq), heads(Wk), heads(Wv))
            att = jax.nn.softmax(jnp.einsum('bhfd,bhgd->bhfg', q, k) / np.sqrt(no), axis=-1)
            o = jnp.einsum('bhfg,bhgd->bhfd', att, v)
            o = o.transpose(0, 2, 1, 3).reshape(Bx, Fx, H * no)
            o = jax.nn.relu(o + jnp.einsum('bfi,oi->bfo', x, Wr))
            mu = jnp.mean(o, axis=-1, keepdims=True)
            var = jnp.mean((o - mu) ** 2, axis=-1, keepdims=True)
            return (o - mu) * jax.lax.rsqrt(var + LN_EPS) * lnw + lnb
        layers = [(Wq0, Wk0, Wv0, Wr0, lnw0, lnb0), (Wq1, Wk1, Wv1, Wr1, lnw1, lnb1), (Wq2, Wk2, Wv2, Wr2, lnw2, lnb2)]
        h = x
        for (Wq, Wk, Wv, Wr, lnw, lnb), nu, nh in zip(layers, NUM_UNITS, NUM_HEADS):
            h = _mha(h, Wq, Wk, Wv, Wr, lnw, lnb, nh, nu)
        flat = h.reshape(h.shape[0], -1)
        return jax.nn.sigmoid(flat @ Wf.T + bf)
    y = _L0_rec_ref(r_x, L0_rec_Wq0, L0_rec_Wk0, L0_rec_Wv0, L0_rec_Wr0, L0_rec_lnw0, L0_rec_lnb0, L0_rec_Wq1, L0_rec_Wk1, L0_rec_Wv1, L0_rec_Wr1, L0_rec_lnw1, L0_rec_lnb1, L0_rec_Wq2, L0_rec_Wk2, L0_rec_Wv2, L0_rec_Wr2, L0_rec_lnw2, L0_rec_lnb2, L0_rec_Wf, L0_rec_bf)
    return y

_drawn_inputs = setup_inputs


def setup_inputs(seed=0):
    import zlib

    import numpy as np

    out = dict(_drawn_inputs(seed))
    spreads = {'L0_rec_lnw0': (1.0, 0.2),
     'L0_rec_lnb0': (0.0, 0.1),
     'L0_rec_lnw1': (1.0, 0.2),
     'L0_rec_lnb1': (0.0, 0.1),
     'L0_rec_lnw2': (1.0, 0.2),
     'L0_rec_lnb2': (0.0, 0.8)}
    factors = {}
    for name, (base, spread) in spreads.items():
        noise = np.random.default_rng([zlib.crc32(name.encode()), seed]).standard_normal(out[name].shape)
        drawn = base * np.exp(spread * noise) if base else spread * noise
        out[name] = jnp.asarray(drawn.astype(out[name].dtype))
    for name, factor in factors.items():
        out[name] = (out[name] * factor).astype(out[name].dtype)
    return out
```

```python
import concourse.bass as bass
from concourse import mybir
from contextlib import ExitStack

B, F, E0, D, H, HD, LAYERS = 512, 40, 64, 128, 2, 64, 3
SPT = 3
P = SPT * F
TILES = 4
SPG = SPT * TILES
TOK = TILES * P
STREAMS = 2
BODY = STREAMS * LAYERS
PASSES = -(-B // (SPG * STREAMS))
UNITS = PASSES * BODY
LAST_START = B - SPG
FULL = B // SPG
GROUPS = PASSES * STREAMS
TH = TILES * H
QW = P
QPAD = P - F
EPS = 1e-5
SCALE = 1.0 / HD ** 0.5


def build(nc, x, wq, wk, wv, wr, lnw, lnb, wf, bf, out):
    f32 = mybir.dt.float32
    ALU = mybir.AluOpType
    ACT = mybir.ActivationFunctionType
    AX = mybir.AxisListType

    ctx = ExitStack()
    with ctx:
        def sb(name, shape, dt=f32):
            return ctx.enter_context(nc.sbuf_tensor(name, shape, dt))

        def pb(name):
            return ctx.enter_context(nc.psum_tensor(name, [128, 512], f32))

        def sem(name):
            return ctx.enter_context(nc.semaphore(name))

        ident = sb("ident", [128, 128])
        in_sample = sb("in_sample", [P, SPT])
        ones = sb("ones", [128, 128])
        minus_half = sb("minus_half", [P, TILES])
        w_raw = sb("w_raw", [D, LAYERS, 4, D])
        w_t = sb("w_t", [D, LAYERS, 4, D])
        ln_w = sb("ln_w", [D, LAYERS])
        ln_b = sb("ln_b", [D, LAYERS])
        wf_rows = sb("wf_rows", [P, D])
        lnw_rows = sb("lnw_rows", [P, D])
        wf_scaled = sb("wf_scaled", [P, D])
        lnb_rows = sb("lnb_rows", [F, D])
        wfb = sb("wfb", [F, D])
        wfb_sum = sb("wfb_sum", [F, 1])
        bf_col = sb("bf_col", [128, 1])
        head_bias = sb("head_bias", [128, 1])

        x_in = sb("x_in", [P, STREAMS, TILES, E0])
        xt = sb("xt", [D, 2, TOK])
        q_pad = sb("q_pad", [D, QPAD + SPG * QW])
        k_diag = sb("k_diag", [D, SPG, H, F])
        v_sb = sb("v_sb", [P, TILES * D])
        smax = sb("smax", [P, TH])
        shifted = sb("shifted", [P, TH, F])
        expd = sb("expd", [P, TH, F])
        ssum = sb("ssum", [P, TH])
        rsum = sb("rsum", [P, TH])
        rsum_own = sb("rsum_own", [P, TH, SPT])
        probs = sb("probs", [P, TH, SPT, F])
        probs_t = sb("probs_t", [P, TH, P])
        o_sb = sb("o_sb", [P, TILES, D])
        stats = sb("stats", [P, TILES, 6])
        mean_var = sb("mean_var", [P, TILES, 2])
        neg_mean = sb("neg_mean", [P, TILES])
        var_eps = sb("var_eps", [P, TILES])
        rstd = sb("rstd", [P, TILES])
        normed = sb("normed", [P, TILES, D])
        weighed = sb("weighed", [P, TILES, D])
        z = sb("z", [P, GROUPS * TILES])
        ZH = GROUPS * TILES // 2
        e_y = sb("e_y", [ZH, 2, SPT])
        d_y = sb("d_y", [ZH, 2, SPT])
        y = sb("y", [ZH, 2, SPT])

        q_ps, k_ps, v_ps, s_ps, pta_ps, ptb_ps, o_ps, xt_ps = (
            pb(n) for n in ("q_ps", "k_ps", "v_ps", "s_ps", "pta_ps", "ptb_ps", "o_ps", "xt_ps"))
        pt_ps = (pta_ps, ptb_ps)

        weights_in = sem("weights_in")
        small_in = sem("small_in")
        masks_zeroed = sem("masks_zeroed")
        masks_built = sem("masks_built")
        pads_zeroed = sem("pads_zeroed")
        wt_ready = sem("wt_ready")
        wt_copied = sem("wt_copied")
        wf_step = sem("wf_step")
        head_bias_ready = sem("head_bias_ready")
        head_bias_copied = sem("head_bias_copied")
        x_loaded = [sem(f"x_loaded{s}") for s in range(STREAMS)]
        xt_ready = sem("xt_ready")
        xt_copied = sem("xt_copied")
        q_ready = sem("q_ready")
        k_ready = sem("k_ready")
        v_ready = sem("v_ready")
        q_copied = sem("q_copied")
        k_copied = sem("k_copied")
        v_copied = sem("v_copied")
        scores_ready = sem("scores_ready")
        max_done = sem("max_done")
        shift_done = sem("shift_done")
        exp_done = sem("exp_done")
        sum_done = sem("sum_done")
        rsum_done = sem("rsum_done")
        rsum_own_done = sem("rsum_own_done")
        probs_done = [sem("probs_a_done"), sem("probs_b_done")]
        pt_ready = [sem("pta_ready"), sem("ptb_ready")]
        pt_copied = [sem("pta_copied"), sem("ptb_copied")]
        o_ready = sem("o_ready")
        relu_done = sem("relu_done")
        stats_done = sem("stats_done")
        mean_var_done = sem("mean_var_done")
        neg_mean_done = sem("neg_mean_done")
        var_eps_done = sem("var_eps_done")
        rstd_done = sem("rstd_done")
        normed_done = sem("normed_done")
        weighed_done = sem("weighed_done")
        z_done = sem("z_done")
        logits_ready = sem("logits_ready")
        head_step = sem("head_step")
        y_exp = sem("y_exp")
        y_ready = sem("y_ready")
        y_written = sem("y_written")
        waits_apart = {e.engine: sem(f"waits_apart_{n}")
                       for n, e in (("pool", nc.gpsimd), ("dve", nc.vector), ("pe", nc.tensor))}

        block = ctx.enter_context(nc.Block())

        def over_units(engine, slot, last):
            for j in range(BODY):
                slot(0, j)
            with engine.Fori(1, PASSES) as i:
                for j in range(BODY):
                    slot(i, j)
            last()

        def unit(i, j):
            return i * BODY + j

        def layer(j):
            return (j % BODY) // STREAMS

        def wait_apart(engine, semaphore, count):
            engine.wait_ge(semaphore, count)
            if not isinstance(count, int):
                engine.sem_inc(waits_apart[engine.engine], 1)

        def before(i, j):
            return (i, j - 1) if j else (i - 1, BODY - 1)

        def normalise(engine, half):
            own = slice(half * TILES, (half + 1) * TILES)
            engine.tensor_tensor(probs[:, own, :, :],
                                 expd[:, own, :].rearrange("p a (s f) -> p a s f", s=1).to_broadcast([P, TILES, SPT, F]),
                                 rsum_own[:, own, :].rearrange("p a (s f) -> p a s f", f=1).to_broadcast([P, TILES, SPT, F]),
                                 ALU.mult).then_inc(probs_done[half], 1)

        @block.sync
        def _(sp):
            for s in range(STREAMS):
                sp.dma_start(x_in[:, s, :, :], x[s * SPG:(s + 1) * SPG].rearrange("(t s) f e -> (s f) t e", t=TILES))\
                    .then_inc(x_loaded[s], 16)
            for l in range(LAYERS):
                for n, w in enumerate((wq, wk, wv, wr)):
                    sp.dma_start(w_raw[:, l, n, 0:w[l].shape[1]], w[l]).then_inc(weights_in, 16)
            with sp.Fori(1, FULL // STREAMS) as i:
                for s in range(STREAMS):
                    sp.wait_ge(xt_ready, unit(i, s) - BODY + 1)
                    sp.dma_start(x_in[:, s, :, :],
                                 x[bass.ds(i * (STREAMS * SPG) + s * SPG, SPG)].rearrange("(t s) f e -> (s f) t e", t=TILES))\
                        .then_inc(x_loaded[s], 16)
            for i in range(FULL // STREAMS, PASSES + 1):
                for s in range(STREAMS if i < PASSES else 1):
                    sp.wait_ge(xt_ready, unit(i, s) - BODY + 1)
                    sp.dma_start(x_in[:, s, :, :], x[LAST_START:B].rearrange("(t s) f e -> (s f) t e", t=TILES))\
                        .then_inc(x_loaded[s], 16)
            sp.wait_ge(y_ready, 1)
            full_rows = FULL * TILES
            done = 0
            for r0, r1, at in ((0, ZH, 0), (ZH, full_rows, ZH * SPT), (full_rows, full_rows + TILES, LAST_START)):
                half = r0 // ZH
                sp.dma_start(out[at:at + (r1 - r0) * SPT, 0].rearrange("(r s) -> r s", s=SPT),
                             y[r0 - half * ZH:r1 - half * ZH, half, :]).then_inc(y_written, 16)
                done += 16
                sp.wait_ge(y_written, done)

        @block.gpsimd
        def _(pool):
            for m in (ident, in_sample):
                pool.memset(m[:], 0.0 if m is ident else 1.0).then_inc(masks_zeroed, 1)
            pool.memset(ones[:], 1.0).then_inc(masks_built, 1)
            pool.memset(minus_half[:], -0.5).then_inc(masks_built, 1)
            pool.wait_ge(masks_zeroed, 2)
            pool.affine_select(out=ident[:], in_=ident[:], compare_op=ALU.not_equal, fill=1.0, base=0,
                               pattern=[[-1, 128]], channel_multiplier=1).then_inc(masks_built, 1)
            pool.affine_select(out=in_sample[:], in_=in_sample[:], compare_op=ALU.is_ge, fill=0.0, base=0,
                               pattern=[[-F, SPT]], channel_multiplier=1).then_inc(masks_zeroed, 1)
            pool.wait_ge(masks_zeroed, 3)
            pool.affine_select(out=in_sample[:], in_=in_sample[:], compare_op=ALU.is_ge, fill=0.0, base=F - 1,
                               pattern=[[F, SPT]], channel_multiplier=-1).then_inc(masks_built, 1)
            pool.wait_ge(small_in, 16 * (2 * LAYERS + SPT + 3))
            pool.tensor_tensor(wf_scaled[:], wf_rows[:], lnw_rows[:], ALU.mult).then_inc(wf_step, 1)
            pool.tensor_tensor(wfb[:], wf_rows[0:F, :], lnb_rows[:], ALU.mult).then_inc(wf_step, 1)
            pool.wait_ge(wf_step, 2)

            def finish(i, j):
                k = unit(i, j)
                wait_apart(pool, mean_var_done, k + 1)
                pool.tensor_scalar(var_eps[:], mean_var[:, :, 1], EPS, None, ALU.add).then_inc(var_eps_done, 1)
                pool.tensor_scalar(neg_mean[:], mean_var[:, :, 0], -1.0, None, ALU.mult).then_inc(neg_mean_done, 1)
                pool.wait_ge(var_eps_done, k + 1)
                pool.tensor_tensor(rstd[:], var_eps[:], minus_half[:], ALU.pow).then_inc(rstd_done, 1)
                pool.wait_ge(neg_mean_done, k + 1)
                wait_apart(pool, rstd_done, k + 1)
                for t in range(TILES):
                    ins = pool.tensor_scalar(normed[:, t, :], o_sb[:, t, :], neg_mean[:, t:t + 1],
                                             rstd[:, t:t + 1], ALU.add, ALU.mult)
                ins.then_inc(normed_done, 1)
                if layer(j) == LAYERS - 1:
                    pool.wait_ge(normed_done, k + 1)
                    pool.tensor_tensor(weighed[:], normed[:],
                                       wf_scaled[:].rearrange("p (a d) -> p a d", a=1).to_broadcast([P, TILES, D]),
                                       ALU.mult).then_inc(weighed_done, 1)

            def slot(i, j):
                k = unit(i, j)
                if not (isinstance(i, int) and k == 0):
                    finish(*before(i, j))
                pool.wait_ge(rsum_own_done, k + 1)
                normalise(pool, 1)

            over_units(pool, slot, lambda: finish(PASSES - 1, BODY - 1))

        @block.scalar
        def _(act):
            for l in range(LAYERS):
                act.dma_start(ln_w[:, l:l + 1], lnw[l].rearrange("(d a) -> d a", a=1)).then_inc(small_in, 16)
                act.dma_start(ln_b[:, l:l + 1], lnb[l].rearrange("(d a) -> d a", a=1)).then_inc(small_in, 16)
            for s in range(SPT):
                act.dma_start(wf_rows[s * F:(s + 1) * F, :], wf[0].rearrange("(f d) -> f d", d=D)).then_inc(small_in, 16)
            last = LAYERS - 1
            act.dma_start(lnw_rows[:], lnw[last].rearrange("(a d) -> a d", a=1).to_broadcast([P, D])).then_inc(small_in, 16)
            act.dma_start(lnb_rows[:], lnb[last].rearrange("(a d) -> a d", a=1).to_broadcast([F, D])).then_inc(small_in, 16)
            act.dma_start(bf_col[:], bf.rearrange("(a d) -> a d", a=1).to_broadcast([128, 1])).then_inc(small_in, 16)
            act.wait_ge(small_in, 16 * (2 * LAYERS + SPT + 3))

            def copy_xt(to, of, src_layer):
                act.wait_ge(xt_ready, to + 1)
                if src_layer is None:
                    act.activation(xt[0:E0, of, :], xt_ps[0:E0, 0:TOK], ACT.Copy).then_inc(xt_copied, 1)
                else:
                    act.activation(xt[:, of, :], xt_ps[:, 0:TOK], ACT.Identity,
                                   scale=ln_w[:, src_layer:src_layer + 1],
                                   bias=ln_b[:, src_layer:src_layer + 1]).then_inc(xt_copied, 1)

            for s in range(STREAMS):
                copy_xt(s, s, None)
            act.wait_ge(pads_zeroed, 2)

            def slot(i, j):
                k = unit(i, j)
                first = isinstance(i, int) and k == 0
                q_view = q_pad[:, QPAD:].rearrange("p (n w) -> p n w", w=QW)[:, :, 0:F]
                act.wait_ge(q_ready, k + 1)
                act.activation(q_view, q_ps[:, 0:TOK].rearrange("p (n f) -> p n f", f=F), ACT.Copy).then_inc(q_copied, 1)
                act.wait_ge(k_ready, k + 1)
                for h in range(H):
                    ins = act.activation(k_diag[h * HD:(h + 1) * HD, :, h, :],
                                         k_ps[h * HD:(h + 1) * HD, 0:TOK].rearrange("p (n f) -> p n f", f=F), ACT.Copy)
                ins.then_inc(k_copied, 1)
                if not first:
                    copy_pt(k - 1)
                    relu(k - 1)
                act.wait_ge(shift_done, k + 1)
                act.activation(expd[:], shifted[:], ACT.Exp, scale=SCALE).then_inc(exp_done, 1)
                act.wait_ge(v_ready, k + 1)
                act.activation(v_sb[:], v_ps[0:P, :], ACT.Copy).then_inc(v_copied, 1)
                if not first:
                    src = layer(j - 1)
                    copy_xt(k + 1, (j + 1) % 2, None if src == LAYERS - 1 else src)

            def copy_pt(k):
                act.wait_ge(pt_ready[1], k + 1)
                act.activation(probs_t[:, TILES:, :], pt_ps[1][0:P, 0:TOK].rearrange("p (a f) -> p a f", f=P), ACT.Copy)\
                    .then_inc(pt_copied[1], 1)

            def relu(k):
                act.wait_ge(o_ready, k + 1)
                if not (isinstance(k, int) and k == 0):
                    act.wait_ge(normed_done, k)
                act.activation(o_sb[:].rearrange("p t d -> p (t d)"), o_ps[0:P, :], ACT.Relu).then_inc(relu_done, 1)

            def last():
                copy_pt(UNITS - 1)
                relu(UNITS - 1)

            over_units(act, slot, last)
            act.wait_ge(logits_ready, 1)
            act.activation(e_y[:], s_ps[0:ZH, 0:2 * SPT].rearrange("p (a s) -> p a s", a=2), ACT.Exp,
                           scale=-1.0, bias=head_bias[0:ZH, :]).then_inc(y_exp, 1)

        @block.vector
        def _(dve):
            dve.memset(q_pad[:], 0.0).then_inc(pads_zeroed, 1)
            dve.memset(k_diag[:].rearrange("p n h f -> p (n h f)"), 0.0).then_inc(pads_zeroed, 1)
            dve.wait_ge(masks_built, 4)
            for l in range(LAYERS):
                dve.wait_ge(wt_ready, l + 1)
                rows = E0 if l == 0 else D
                dve.tensor_copy(w_t[0:rows, l, :, :].rearrange("p n d -> p (n d)"), (s_ps, o_ps, q_ps)[l][0:rows, :])\
                    .then_inc(wt_copied, 1)
            dve.wait_ge(wf_step, 2)
            dve.tensor_reduce(wfb_sum[:], wfb[:], AX.X, ALU.add).then_inc(wf_step, 1)
            dve.wait_ge(head_bias_ready, 1)
            dve.tensor_scalar(head_bias[:], k_ps[:, 0:1], bf_col[:, 0:1], -1.0, ALU.add, ALU.mult)\
                .then_inc(head_bias_copied, 1)

            def copy_pt(k):
                dve.wait_ge(pt_ready[0], k + 1)
                dve.tensor_copy(probs_t[:, 0:TILES, :], pt_ps[0][0:P, 0:TOK].rearrange("p (a f) -> p a f", f=P))\
                    .then_inc(pt_copied[0], 1)

            def moments(k):
                dve.wait_ge(relu_done, k + 1)
                for t in range(TILES):
                    ins = dve.bn_stats(stats[:, t, :], o_sb[:, t, :])
                ins.then_inc(stats_done, 1)
                wait_apart(dve, stats_done, k + 1)
                for t in range(TILES):
                    ins = dve.bn_aggr(mean_var[:, t, :], stats[:, t, :])
                ins.then_inc(mean_var_done, 1)

            def read_out(i, j):
                group = i * STREAMS + j % STREAMS
                dve.wait_ge(weighed_done, group + 1)
                dve.tensor_reduce(z[:, bass.ds(group * TILES, TILES)], weighed[:], AX.X, ALU.add).then_inc(z_done, 1)

            def slot(i, j):
                k = unit(i, j)
                first = isinstance(i, int) and k == 0
                if not first:
                    copy_pt(k - 1)
                    moments(k - 1)
                dve.wait_ge(scores_ready, k + 1)
                s_view = s_ps[0:P, 0:TH * F].rearrange("p (a f) -> p a f", f=F)
                dve.tensor_reduce(smax[:], s_view, AX.X, ALU.max).then_inc(max_done, 1)
                dve.wait_ge(max_done, k + 1)
                dve.tensor_tensor(shifted[:], s_view,
                                  smax[:].rearrange("p (a b) -> p a b", b=1).to_broadcast([P, TH, F]),
                                  ALU.subtract).then_inc(shift_done, 1)
                dve.wait_ge(exp_done, k + 1)
                dve.tensor_reduce(ssum[:], expd[:], AX.X, ALU.add).then_inc(sum_done, 1)
                dve.wait_ge(sum_done, k + 1)
                dve.reciprocal(rsum[:], ssum[:]).then_inc(rsum_done, 1)
                dve.wait_ge(rsum_done, k + 1)
                dve.tensor_tensor(rsum_own[:],
                                  rsum[:].rearrange("p (a b) -> p a b", b=1).to_broadcast([P, TH, SPT]),
                                  in_sample[:].rearrange("p (a b) -> p a b", a=1).to_broadcast([P, TH, SPT]),
                                  ALU.mult).then_inc(rsum_own_done, 1)
                dve.wait_ge(rsum_own_done, k + 1)
                normalise(dve, 0)
                if not first and layer(j - 1) == LAYERS - 1:
                    read_out(*before(i, j))

            def last():
                copy_pt(UNITS - 1)
                moments(UNITS - 1)
                read_out(PASSES - 1, BODY - 1)

            over_units(dve, slot, last)
            dve.wait_ge(y_exp, 1)
            dve.tensor_scalar(d_y[:], e_y[:], 1.0, None, ALU.add).then_inc(head_step, 1)
            dve.wait_ge(head_step, 1)
            dve.reciprocal(y[:], d_y[:]).then_inc(y_ready, 1)

        @block.tensor
        def _(pe):
            pe.wait_ge(masks_built, 4)

            def transpose_x(to, stream, loaded):
                wait_apart(pe, x_loaded[stream], loaded)
                for t in range(TILES):
                    ins = pe.transpose(xt_ps[0:E0, t * P:(t + 1) * P], x_in[:, stream, t, :], ident[0:P, 0:P])
                ins.then_inc(xt_ready, 1)

            for s in range(STREAMS):
                if s:
                    pe.wait_ge(xt_copied, s)
                transpose_x(s, s, 16)
            pe.wait_ge(weights_in, 16 * 4 * LAYERS)
            for l in range(LAYERS):
                rows = E0 if l == 0 else D
                for n in range(4):
                    ins = pe.transpose((s_ps, o_ps, q_ps)[l][0:rows, n * D:(n + 1) * D],
                                       w_raw[:, l, n, 0:rows], ident[:])
                ins.then_inc(wt_ready, 1)
            pe.wait_ge(wf_step, 3)
            pe.matmul(k_ps[:, 0:1], ones[0:F, :], wfb_sum[:], start=True, stop=True).then_inc(head_bias_ready, 1)
            pe.wait_ge(wt_copied, LAYERS)
            pe.wait_ge(head_bias_copied, 1)

            def project_qk(k, j):
                rows = E0 if layer(j) == 0 else D
                pe.wait_ge(xt_copied, k + 1)
                pe.matmul(q_ps[:, 0:TOK], w_t[0:rows, layer(j), 0, :], xt[0:rows, j % 2, :], start=True, stop=True)\
                    .then_inc(q_ready, 1)
                pe.matmul(k_ps[:, 0:TOK], w_t[0:rows, layer(j), 1, :], xt[0:rows, j % 2, :], start=True, stop=True)\
                    .then_inc(k_ready, 1)

            def scores(k):
                pe.wait_ge(q_copied, k + 1)
                pe.wait_ge(k_copied, k + 1)
                for t in range(TILES):
                    for s in range(SPT):
                        n = t * SPT + s
                        at = QPAD + n * QW - s * F
                        ins = pe.matmul(s_ps[0:P, t * H * F:(t + 1) * H * F], q_pad[:, at:at + P],
                                        k_diag[:, n, :, :].rearrange("p h f -> p (h f)"),
                                        start=(s == 0), stop=(s == SPT - 1))
                ins.then_inc(scores_ready, 1)

            def project_v(k, j):
                rows = E0 if layer(j) == 0 else D
                for t in range(TILES):
                    ins = pe.matmul(v_ps[0:P, t * D:(t + 1) * D], xt[0:rows, j % 2, t * P:(t + 1) * P],
                                    w_t[0:rows, layer(j), 2, :], start=True, stop=True)
                ins.then_inc(v_ready, 1)

            def project_r(k, j, first):
                rows = E0 if layer(j) == 0 else D
                if not first:
                    pe.wait_ge(relu_done, k)
                for t in range(TILES):
                    pe.matmul(o_ps[0:P, t * D:(t + 1) * D], xt[0:rows, j % 2, t * P:(t + 1) * P],
                              w_t[0:rows, layer(j), 3, :], start=(t == 0), stop=False, skip_group_check=True)

            def attend(k):
                for half in range(2):
                    pe.wait_ge(probs_done[half], k + 1)
                    for a in range(TILES):
                        src = probs[:, half * TILES + a, :, :].rearrange("p s f -> p (s f)")
                        ins = pe.transpose(pt_ps[half][0:P, a * P:(a + 1) * P], src, ident[0:P, 0:P])
                    ins.then_inc(pt_ready[half], 1)
                pe.wait_ge(v_copied, k + 1)
                for half in range(2):
                    pe.wait_ge(pt_copied[half], k + 1)
                    for a in range(TILES):
                        th = half * TILES + a
                        ins = pe.matmul(o_ps[0:P, th * HD:(th + 1) * HD], probs_t[:, th, :],
                                        v_sb[:, th * HD:(th + 1) * HD], start=False, stop=True, skip_group_check=True)
                ins.then_inc(o_ready, 1)

            def slot(i, j):
                k = unit(i, j)
                first = isinstance(i, int) and k == 0
                project_qk(k, j)
                if not first:
                    attend(k - 1)
                scores(k)
                project_v(k, j)
                if not first:
                    if layer(j - 1) == LAYERS - 1:
                        stream = (j + 1) % STREAMS
                        group_pass = i + (1 if j == BODY - 1 else 0)
                        transpose_x(k + 1, stream, 16 * group_pass + 16)
                    else:
                        pe.wait_ge(normed_done, k)
                        for t in range(TILES):
                            ins = pe.transpose(xt_ps[:, t * P:(t + 1) * P], normed[:, t, :], ident[0:P, 0:P])
                        ins.then_inc(xt_ready, 1)
                project_r(k, j, first)

            over_units(pe, slot, lambda: attend(UNITS - 1))
            pe.wait_ge(z_done, GROUPS)
            for half in range(2):
                ins = pe.matmul(s_ps[0:ZH, half * SPT:(half + 1) * SPT], z[:, half * ZH:(half + 1) * ZH],
                                in_sample[:], start=True, stop=True)
            ins.then_inc(logits_ready, 1)


_PRE = "L0_rec_"
_INS = ["r_x"] + [_PRE + n + str(l) for n in ("Wq", "Wk", "Wv", "Wr", "lnw", "lnb") for l in range(LAYERS)] + \
    [_PRE + "Wf", _PRE + "bf"]


def kernel(**inputs):
    import numpy as _np
    import concourse.bacc as _bacc
    from concourse import mybir as _mybir
    from concourse.bass_utils import run_bass_kernel_spmd as _run

    nc = _bacc.Bacc("TRN2", target_bir_lowering=False, num_devices=1)
    arrays, aps = {}, {}
    for name in _INS:
        a = _np.ascontiguousarray(inputs[name])
        arrays[f"in_{name}"] = a
        aps[name] = nc.dram_tensor(f"in_{name}", a.shape, _mybir.dt.from_np(a.dtype), kind="ExternalInput").ap()
    out = nc.dram_tensor("out_y", (B, 1), _mybir.dt.float32, kind="ExternalOutput").ap()
    per_layer = [[aps[_PRE + n + str(l)] for l in range(LAYERS)] for n in ("Wq", "Wk", "Wv", "Wr", "lnw", "lnb")]
    build(nc, aps["r_x"], *per_layer, aps[_PRE + "Wf"], aps[_PRE + "bf"], out)
    r = _run(nc, [arrays], core_ids=[0])
    return r.results[0]["out_y"]
```

```python
import concourse.bass as bass
from concourse import mybir
from contextlib import ExitStack

B, F, E0, D, H, HD, LAYERS = 512, 40, 64, 128, 2, 64, 3
SPT = 3
P = SPT * F
TILES = 4
SPG = SPT * TILES
TOK = TILES * P
STREAMS = 3
BODY = STREAMS * LAYERS
PASSES = -(-B // (SPG * STREAMS))
UNITS = PASSES * BODY
LAST_START = B - SPG
FULL = B // SPG
GROUPS = PASSES * STREAMS
TH = TILES * H
QW = P
QPAD = P - F
EPS = 1e-5
SCALE = 1.0 / HD ** 0.5


def build(nc, x, wq, wk, wv, wr, lnw, lnb, wf, bf, out):
    f32 = mybir.dt.float32
    ALU = mybir.AluOpType
    ACT = mybir.ActivationFunctionType
    AX = mybir.AxisListType

    ctx = ExitStack()
    with ctx:
        def sb(name, shape, dt=f32):
            return ctx.enter_context(nc.sbuf_tensor(name, shape, dt))

        def pb(name):
            return ctx.enter_context(nc.psum_tensor(name, [128, 512], f32))

        def sem(name):
            return ctx.enter_context(nc.semaphore(name))

        ident = sb("ident", [128, 128])
        in_sample = sb("in_sample", [P, SPT])
        ones = sb("ones", [128, 128])
        minus_half = sb("minus_half", [P, TILES])
        w_raw = sb("w_raw", [D, LAYERS, 4, D])
        w_t = sb("w_t", [D, LAYERS, 4, D])
        ln_w = sb("ln_w", [D, LAYERS])
        ln_b = sb("ln_b", [D, LAYERS])
        wf_rows = sb("wf_rows", [P, D])
        lnw_rows = sb("lnw_rows", [P, D])
        wf_scaled = sb("wf_scaled", [P, D])
        lnb_rows = sb("lnb_rows", [F, D])
        wfb = sb("wfb", [F, D])
        wfb_sum = sb("wfb_sum", [F, 1])
        bf_col = sb("bf_col", [128, 1])
        head_bias = sb("head_bias", [128, 1])

        x_in = sb("x_in", [P, STREAMS, TILES, E0])
        xt = sb("xt", [D, STREAMS, TOK])
        q_pad = sb("q_pad", [D, QPAD + SPG * QW])
        k_diag = sb("k_diag", [D, SPG, H, F])
        v_sb = sb("v_sb", [P, STREAMS, TILES * D])
        smax = sb("smax", [P, TH])
        shifted = sb("shifted", [P, TH, F])
        expd = sb("expd", [P, TH, F])
        ssum = sb("ssum", [P, TH])
        rsum = sb("rsum", [P, TH])
        rsum_own = sb("rsum_own", [P, TH, SPT])
        probs = sb("probs", [P, TH, SPT, F])
        probs_t = sb("probs_t", [P, TH, P])
        o_sb = sb("o_sb", [P, TILES, D])
        stats = sb("stats", [P, TILES, 6])
        mean_var = sb("mean_var", [P, TILES, 2])
        neg_mean = sb("neg_mean", [P, TILES])
        var_eps = sb("var_eps", [P, TILES])
        rstd = sb("rstd", [P, TILES])
        normed = sb("normed", [P, TILES, D])
        weighed = sb("weighed", [P, TILES, D])
        z = sb("z", [P, GROUPS * TILES])
        ZH = GROUPS * TILES // 2
        e_y = sb("e_y", [ZH, 2, SPT])
        d_y = sb("d_y", [ZH, 2, SPT])
        y = sb("y", [ZH, 2, SPT])

        q_ps, k_ps, v_ps, s_ps, pta_ps, ptb_ps, o_ps, xt_ps = (
            pb(n) for n in ("q_ps", "k_ps", "v_ps", "s_ps", "pta_ps", "ptb_ps", "o_ps", "xt_ps"))
        pt_ps = (pta_ps, ptb_ps)

        weights_in = sem("weights_in")
        small_in = sem("small_in")
        masks_zeroed = sem("masks_zeroed")
        masks_built = sem("masks_built")
        pads_zeroed = sem("pads_zeroed")
        wt_ready = sem("wt_ready")
        wt_copied = sem("wt_copied")
        wf_step = sem("wf_step")
        head_bias_ready = sem("head_bias_ready")
        head_bias_copied = sem("head_bias_copied")
        x_loaded = [sem(f"x_loaded{s}") for s in range(STREAMS)]
        xt_ready = sem("xt_ready")
        xt_copied = sem("xt_copied")
        q_ready = sem("q_ready")
        k_ready = sem("k_ready")
        v_ready = sem("v_ready")
        q_copied = sem("q_copied")
        k_copied = sem("k_copied")
        v_copied = sem("v_copied")
        scores_ready = sem("scores_ready")
        max_done = sem("max_done")
        shift_done = sem("shift_done")
        exp_done = sem("exp_done")
        sum_done = sem("sum_done")
        rsum_done = sem("rsum_done")
        rsum_own_done = sem("rsum_own_done")
        probs_done = [sem("probs_a_done"), sem("probs_b_done")]
        pt_ready = [sem("pta_ready"), sem("ptb_ready")]
        pt_copied = [sem("pta_copied"), sem("ptb_copied")]
        o_ready = sem("o_ready")
        relu_done = sem("relu_done")
        stats_done = sem("stats_done")
        mean_var_done = sem("mean_var_done")
        neg_mean_done = sem("neg_mean_done")
        var_eps_done = sem("var_eps_done")
        rstd_done = sem("rstd_done")
        normed_done = sem("normed_done")
        weighed_done = sem("weighed_done")
        z_done = sem("z_done")
        logits_ready = sem("logits_ready")
        head_step = sem("head_step")
        y_exp = sem("y_exp")
        y_ready = sem("y_ready")
        y_written = sem("y_written")
        waits_apart = {e.engine: sem(f"waits_apart_{n}")
                       for n, e in (("pool", nc.gpsimd), ("dve", nc.vector), ("pe", nc.tensor))}

        block = ctx.enter_context(nc.Block())

        def over_units(engine, slot, last):
            for j in range(BODY):
                slot(0, j)
            with engine.Fori(1, PASSES) as i:
                for j in range(BODY):
                    slot(i, j)
            last()

        def unit(i, j):
            return i * BODY + j

        def layer(j):
            return (j % BODY) // STREAMS

        def wait_apart(engine, semaphore, count):
            engine.wait_ge(semaphore, count)
            if not isinstance(count, int):
                engine.sem_inc(waits_apart[engine.engine], 1)

        def before(i, j, by=1):
            return (i, j - by) if j >= by else (i - 1, j - by + BODY)

        def exists(i, j, by=1):
            return not (isinstance(i, int) and i == 0 and j < by)

        def normalise(engine, half):
            own = slice(half * TILES, (half + 1) * TILES)
            engine.tensor_tensor(probs[:, own, :, :],
                                 expd[:, own, :].rearrange("p a (s f) -> p a s f", s=1).to_broadcast([P, TILES, SPT, F]),
                                 rsum_own[:, own, :].rearrange("p a (s f) -> p a s f", f=1).to_broadcast([P, TILES, SPT, F]),
                                 ALU.mult).then_inc(probs_done[half], 1)

        @block.sync
        def _(sp):
            for s in range(STREAMS):
                sp.dma_start(x_in[:, s, :, :], x[s * SPG:(s + 1) * SPG].rearrange("(t s) f e -> (s f) t e", t=TILES))\
                    .then_inc(x_loaded[s], 16)
            for l in range(LAYERS):
                for n, w in enumerate((wq, wk, wv, wr)):
                    sp.dma_start(w_raw[:, l, n, 0:w[l].shape[1]], w[l]).then_inc(weights_in, 16)
            with sp.Fori(1, FULL // STREAMS) as i:
                for s in range(STREAMS):
                    sp.wait_ge(xt_ready, unit(i, s) - BODY + 1)
                    sp.dma_start(x_in[:, s, :, :],
                                 x[bass.ds(i * (STREAMS * SPG) + s * SPG, SPG)].rearrange("(t s) f e -> (s f) t e", t=TILES))\
                        .then_inc(x_loaded[s], 16)
            for i in range(FULL // STREAMS, PASSES + 1):
                for s in range(STREAMS if i < PASSES else 1):
                    sp.wait_ge(xt_ready, unit(i, s) - BODY + 1)
                    sp.dma_start(x_in[:, s, :, :], x[LAST_START:B].rearrange("(t s) f e -> (s f) t e", t=TILES))\
                        .then_inc(x_loaded[s], 16)
            sp.wait_ge(y_ready, 1)
            full_rows = FULL * TILES
            done = 0
            for r0, r1, at in ((0, ZH, 0), (ZH, full_rows, ZH * SPT), (full_rows, full_rows + TILES, LAST_START)):
                half = r0 // ZH
                sp.dma_start(out[at:at + (r1 - r0) * SPT, 0].rearrange("(r s) -> r s", s=SPT),
                             y[r0 - half * ZH:r1 - half * ZH, half, :]).then_inc(y_written, 16)
                done += 16
                sp.wait_ge(y_written, done)

        @block.gpsimd
        def _(pool):
            for m in (ident, in_sample):
                pool.memset(m[:], 0.0 if m is ident else 1.0).then_inc(masks_zeroed, 1)
            pool.memset(ones[:], 1.0).then_inc(masks_built, 1)
            pool.memset(minus_half[:], -0.5).then_inc(masks_built, 1)
            pool.wait_ge(masks_zeroed, 2)
            pool.affine_select(out=ident[:], in_=ident[:], compare_op=ALU.not_equal, fill=1.0, base=0,
                               pattern=[[-1, 128]], channel_multiplier=1).then_inc(masks_built, 1)
            pool.affine_select(out=in_sample[:], in_=in_sample[:], compare_op=ALU.is_ge, fill=0.0, base=0,
                               pattern=[[-F, SPT]], channel_multiplier=1).then_inc(masks_zeroed, 1)
            pool.wait_ge(masks_zeroed, 3)
            pool.affine_select(out=in_sample[:], in_=in_sample[:], compare_op=ALU.is_ge, fill=0.0, base=F - 1,
                               pattern=[[F, SPT]], channel_multiplier=-1).then_inc(masks_built, 1)
            pool.wait_ge(small_in, 16 * (2 * LAYERS + SPT + 3))
            pool.tensor_tensor(wf_scaled[:], wf_rows[:], lnw_rows[:], ALU.mult).then_inc(wf_step, 1)
            pool.tensor_tensor(wfb[:], wf_rows[0:F, :], lnb_rows[:], ALU.mult).then_inc(wf_step, 1)
            pool.wait_ge(wf_step, 2)

            def finish(i, j):
                k = unit(i, j)
                wait_apart(pool, mean_var_done, k + 1)
                pool.tensor_scalar(var_eps[:], mean_var[:, :, 1], EPS, None, ALU.add).then_inc(var_eps_done, 1)
                pool.tensor_scalar(neg_mean[:], mean_var[:, :, 0], -1.0, None, ALU.mult).then_inc(neg_mean_done, 1)
                pool.wait_ge(var_eps_done, k + 1)
                pool.tensor_tensor(rstd[:], var_eps[:], minus_half[:], ALU.pow).then_inc(rstd_done, 1)
                pool.wait_ge(neg_mean_done, k + 1)
                wait_apart(pool, rstd_done, k + 1)
                for t in range(TILES):
                    ins = pool.tensor_scalar(normed[:, t, :], o_sb[:, t, :], neg_mean[:, t:t + 1],
                                             rstd[:, t:t + 1], ALU.add, ALU.mult)
                ins.then_inc(normed_done, 1)
                if layer(j) == LAYERS - 1:
                    pool.wait_ge(normed_done, k + 1)
                    group = i * STREAMS + j % STREAMS
                    if not (isinstance(group, int) and group == 0):
                        pool.wait_ge(z_done, group)
                    pool.tensor_tensor(weighed[:], normed[:],
                                       wf_scaled[:].rearrange("p (a d) -> p a d", a=1).to_broadcast([P, TILES, D]),
                                       ALU.mult).then_inc(weighed_done, 1)

            def slot(i, j):
                pool.wait_ge(rsum_own_done, unit(i, j) + 1)
                normalise(pool, 1)
                if exists(i, j):
                    finish(*before(i, j))

            over_units(pool, slot, lambda: finish(PASSES - 1, BODY - 1))

        @block.scalar
        def _(act):
            for l in range(LAYERS):
                act.dma_start(ln_w[:, l:l + 1], lnw[l].rearrange("(d a) -> d a", a=1)).then_inc(small_in, 16)
                act.dma_start(ln_b[:, l:l + 1], lnb[l].rearrange("(d a) -> d a", a=1)).then_inc(small_in, 16)
            for s in range(SPT):
                act.dma_start(wf_rows[s * F:(s + 1) * F, :], wf[0].rearrange("(f d) -> f d", d=D)).then_inc(small_in, 16)
            last = LAYERS - 1
            act.dma_start(lnw_rows[:], lnw[last].rearrange("(a d) -> a d", a=1).to_broadcast([P, D])).then_inc(small_in, 16)
            act.dma_start(lnb_rows[:], lnb[last].rearrange("(a d) -> a d", a=1).to_broadcast([F, D])).then_inc(small_in, 16)
            act.dma_start(bf_col[:], bf.rearrange("(a d) -> a d", a=1).to_broadcast([128, 1])).then_inc(small_in, 16)
            act.wait_ge(small_in, 16 * (2 * LAYERS + SPT + 3))

            def copy_xt(to, stream, src_layer):
                act.wait_ge(xt_ready, to + 1)
                if src_layer is None:
                    act.activation(xt[0:E0, stream, :], xt_ps[0:E0, 0:TOK], ACT.Copy).then_inc(xt_copied, 1)
                else:
                    act.activation(xt[:, stream, :], xt_ps[:, 0:TOK], ACT.Identity,
                                   scale=ln_w[:, src_layer:src_layer + 1],
                                   bias=ln_b[:, src_layer:src_layer + 1]).then_inc(xt_copied, 1)

            copy_xt(0, 0, None)
            act.wait_ge(pads_zeroed, 2)

            def slot(i, j):
                k = unit(i, j)
                q_view = q_pad[:, QPAD:].rearrange("p (n w) -> p n w", w=QW)[:, :, 0:F]
                act.wait_ge(q_ready, k + 1)
                act.activation(q_view, q_ps[:, 0:TOK].rearrange("p (n f) -> p n f", f=F), ACT.Copy).then_inc(q_copied, 1)
                act.wait_ge(k_ready, k + 1)
                for h in range(H):
                    ins = act.activation(k_diag[h * HD:(h + 1) * HD, :, h, :],
                                         k_ps[h * HD:(h + 1) * HD, 0:TOK].rearrange("p (n f) -> p n f", f=F), ACT.Copy)
                ins.then_inc(k_copied, 1)
                act.wait_ge(v_ready, k + 1)
                act.activation(v_sb[:, j % STREAMS, :], v_ps[0:P, :], ACT.Copy).then_inc(v_copied, 1)
                if exists(i, j):
                    copy_pt(k - 1)
                src = layer(j - 2)
                copy_xt(k + 1, (j + 1) % STREAMS, None if src == LAYERS - 1 else src)
                act.wait_ge(shift_done, k + 1)
                act.activation(expd[:], shifted[:], ACT.Exp, scale=SCALE).then_inc(exp_done, 1)
                if exists(i, j):
                    relu(k - 1)

            def copy_pt(k):
                act.wait_ge(pt_ready[1], k + 1)
                act.activation(probs_t[:, TILES:, :], pt_ps[1][0:P, 0:TOK].rearrange("p (a f) -> p a f", f=P), ACT.Copy)\
                    .then_inc(pt_copied[1], 1)

            def relu(k):
                act.wait_ge(o_ready, k + 1)
                if not (isinstance(k, int) and k == 0):
                    act.wait_ge(normed_done, k)
                act.activation(o_sb[:].rearrange("p t d -> p (t d)"), o_ps[0:P, :], ACT.Relu).then_inc(relu_done, 1)

            def last():
                copy_pt(UNITS - 1)
                relu(UNITS - 1)

            over_units(act, slot, last)
            act.wait_ge(logits_ready, 1)
            act.activation(e_y[:], s_ps[0:ZH, 0:2 * SPT].rearrange("p (a s) -> p a s", a=2), ACT.Exp,
                           scale=-1.0, bias=head_bias[0:ZH, :]).then_inc(y_exp, 1)

        @block.vector
        def _(dve):
            dve.memset(q_pad[:], 0.0).then_inc(pads_zeroed, 1)
            dve.memset(k_diag[:].rearrange("p n h f -> p (n h f)"), 0.0).then_inc(pads_zeroed, 1)
            dve.wait_ge(masks_built, 4)
            for l in range(LAYERS):
                dve.wait_ge(wt_ready, l + 1)
                rows = E0 if l == 0 else D
                dve.tensor_copy(w_t[0:rows, l, :, :].rearrange("p n d -> p (n d)"), (s_ps, o_ps, q_ps)[l][0:rows, :])\
                    .then_inc(wt_copied, 1)
            dve.wait_ge(wf_step, 2)
            dve.tensor_reduce(wfb_sum[:], wfb[:], AX.X, ALU.add).then_inc(wf_step, 1)
            dve.wait_ge(head_bias_ready, 1)
            dve.tensor_scalar(head_bias[:], k_ps[:, 0:1], bf_col[:, 0:1], -1.0, ALU.add, ALU.mult)\
                .then_inc(head_bias_copied, 1)

            def copy_pt(k):
                dve.wait_ge(pt_ready[0], k + 1)
                dve.tensor_copy(probs_t[:, 0:TILES, :], pt_ps[0][0:P, 0:TOK].rearrange("p (a f) -> p a f", f=P))\
                    .then_inc(pt_copied[0], 1)

            def moments(k):
                dve.wait_ge(relu_done, k + 1)
                for t in range(TILES):
                    ins = dve.bn_stats(stats[:, t, :], o_sb[:, t, :])
                ins.then_inc(stats_done, 1)
                wait_apart(dve, stats_done, k + 1)
                for t in range(TILES):
                    ins = dve.bn_aggr(mean_var[:, t, :], stats[:, t, :])
                ins.then_inc(mean_var_done, 1)

            def read_out(i, j):
                group = i * STREAMS + j % STREAMS
                dve.wait_ge(weighed_done, group + 1)
                dve.tensor_reduce(z[:, bass.ds(group * TILES, TILES)], weighed[:], AX.X, ALU.add).then_inc(z_done, 1)

            def slot(i, j):
                k = unit(i, j)
                if exists(i, j):
                    copy_pt(k - 1)
                dve.wait_ge(scores_ready, k + 1)
                s_view = s_ps[0:P, 0:TH * F].rearrange("p (a f) -> p a f", f=F)
                dve.tensor_reduce(smax[:], s_view, AX.X, ALU.max).then_inc(max_done, 1)
                dve.wait_ge(max_done, k + 1)
                dve.tensor_tensor(shifted[:], s_view,
                                  smax[:].rearrange("p (a b) -> p a b", b=1).to_broadcast([P, TH, F]),
                                  ALU.subtract).then_inc(shift_done, 1)
                dve.wait_ge(exp_done, k + 1)
                dve.tensor_reduce(ssum[:], expd[:], AX.X, ALU.add).then_inc(sum_done, 1)
                dve.wait_ge(sum_done, k + 1)
                dve.reciprocal(rsum[:], ssum[:]).then_inc(rsum_done, 1)
                dve.wait_ge(rsum_done, k + 1)
                dve.tensor_tensor(rsum_own[:],
                                  rsum[:].rearrange("p (a b) -> p a b", b=1).to_broadcast([P, TH, SPT]),
                                  in_sample[:].rearrange("p (a b) -> p a b", a=1).to_broadcast([P, TH, SPT]),
                                  ALU.mult).then_inc(rsum_own_done, 1)
                dve.wait_ge(rsum_own_done, k + 1)
                normalise(dve, 0)
                if exists(i, j):
                    moments(k - 1)
                if exists(i, j, 2) and layer(j - 2) == LAYERS - 1:
                    read_out(*before(i, j, 2))

            def last():
                copy_pt(UNITS - 1)
                moments(UNITS - 1)
                read_out(PASSES - 1, BODY - 2)
                read_out(PASSES - 1, BODY - 1)

            over_units(dve, slot, last)
            dve.wait_ge(y_exp, 1)
            dve.tensor_scalar(d_y[:], e_y[:], 1.0, None, ALU.add).then_inc(head_step, 1)
            dve.wait_ge(head_step, 1)
            dve.reciprocal(y[:], d_y[:]).then_inc(y_ready, 1)

        @block.tensor
        def _(pe):
            pe.wait_ge(masks_built, 4)

            def transpose_x(to, stream, loaded):
                wait_apart(pe, x_loaded[stream], loaded)
                for t in range(TILES):
                    ins = pe.transpose(xt_ps[0:E0, t * P:(t + 1) * P], x_in[:, stream, t, :], ident[0:P, 0:P])
                ins.then_inc(xt_ready, 1)

            transpose_x(0, 0, 16)
            pe.wait_ge(weights_in, 16 * 4 * LAYERS)
            for l in range(LAYERS):
                rows = E0 if l == 0 else D
                for n in range(4):
                    ins = pe.transpose((s_ps, o_ps, q_ps)[l][0:rows, n * D:(n + 1) * D],
                                       w_raw[:, l, n, 0:rows], ident[:])
                ins.then_inc(wt_ready, 1)
            pe.wait_ge(wf_step, 3)
            pe.matmul(k_ps[:, 0:1], ones[0:F, :], wfb_sum[:], start=True, stop=True).then_inc(head_bias_ready, 1)
            pe.wait_ge(wt_copied, LAYERS)
            pe.wait_ge(head_bias_copied, 1)

            def project_qk(k, j):
                rows = E0 if layer(j) == 0 else D
                pe.wait_ge(xt_copied, k + 1)
                pe.matmul(q_ps[:, 0:TOK], w_t[0:rows, layer(j), 0, :], xt[0:rows, j % STREAMS, :], start=True, stop=True)\
                    .then_inc(q_ready, 1)
                pe.matmul(k_ps[:, 0:TOK], w_t[0:rows, layer(j), 1, :], xt[0:rows, j % STREAMS, :], start=True, stop=True)\
                    .then_inc(k_ready, 1)

            def scores(k):
                pe.wait_ge(q_copied, k + 1)
                pe.wait_ge(k_copied, k + 1)
                for t in range(TILES):
                    for s in range(SPT):
                        n = t * SPT + s
                        at = QPAD + n * QW - s * F
                        ins = pe.matmul(s_ps[0:P, t * H * F:(t + 1) * H * F], q_pad[:, at:at + P],
                                        k_diag[:, n, :, :].rearrange("p h f -> p (h f)"),
                                        start=(s == 0), stop=(s == SPT - 1))
                ins.then_inc(scores_ready, 1)

            def project_v(k, j):
                rows = E0 if layer(j) == 0 else D
                if not (isinstance(k, int) and k == 0):
                    pe.wait_ge(v_copied, k)
                for t in range(TILES):
                    ins = pe.matmul(v_ps[0:P, t * D:(t + 1) * D], xt[0:rows, j % STREAMS, t * P:(t + 1) * P],
                                    w_t[0:rows, layer(j), 2, :], start=True, stop=True)
                ins.then_inc(v_ready, 1)

            def project_r(k, j):
                rows = E0 if layer(j) == 0 else D
                if not (isinstance(k, int) and k == 0):
                    pe.wait_ge(relu_done, k)
                for t in range(TILES):
                    pe.matmul(o_ps[0:P, t * D:(t + 1) * D], xt[0:rows, j % STREAMS, t * P:(t + 1) * P],
                              w_t[0:rows, layer(j), 3, :], start=(t == 0), stop=False, skip_group_check=True)

            def transpose_probs(k):
                for half in range(2):
                    pe.wait_ge(probs_done[half], k + 1)
                    for a in range(TILES):
                        src = probs[:, half * TILES + a, :, :].rearrange("p s f -> p (s f)")
                        ins = pe.transpose(pt_ps[half][0:P, a * P:(a + 1) * P], src, ident[0:P, 0:P])
                    ins.then_inc(pt_ready[half], 1)

            def attend(k, j):
                pe.wait_ge(v_copied, k + 1)
                for half in range(2):
                    pe.wait_ge(pt_copied[half], k + 1)
                    for a in range(TILES):
                        th = half * TILES + a
                        ins = pe.matmul(o_ps[0:P, th * HD:(th + 1) * HD], probs_t[:, th, :],
                                        v_sb[:, j % STREAMS, th * HD:(th + 1) * HD], start=False, stop=True, skip_group_check=True)
                ins.then_inc(o_ready, 1)

            def transpose_input(i, j):
                k = unit(i, j)
                if layer(j - 2) == LAYERS - 1:
                    group_pass = i + (1 if j == BODY - 1 else 0)
                    transpose_x(k + 1, (j + 1) % STREAMS, 16 * group_pass + 16)
                else:
                    pe.wait_ge(normed_done, k - 1)
                    for t in range(TILES):
                        ins = pe.transpose(xt_ps[:, t * P:(t + 1) * P], normed[:, t, :], ident[0:P, 0:P])
                    ins.then_inc(xt_ready, 1)

            def slot(i, j):
                k = unit(i, j)
                project_qk(k, j)
                if exists(i, j):
                    project_r(k - 1, j - 1)
                project_v(k, j)
                if exists(i, j):
                    transpose_probs(k - 1)
                scores(k)
                transpose_input(i, j)
                if exists(i, j):
                    attend(k - 1, j - 1)

            def last():
                project_r(UNITS - 1, BODY - 1)
                transpose_probs(UNITS - 1)
                attend(UNITS - 1, BODY - 1)

            over_units(pe, slot, last)
            pe.wait_ge(z_done, GROUPS)
            for half in range(2):
                ins = pe.matmul(s_ps[0:ZH, half * SPT:(half + 1) * SPT], z[:, half * ZH:(half + 1) * ZH],
                                in_sample[:], start=True, stop=True)
            ins.then_inc(logits_ready, 1)


_PRE = "L0_rec_"
_INS = ["r_x"] + [_PRE + n + str(l) for n in ("Wq", "Wk", "Wv", "Wr", "lnw", "lnb") for l in range(LAYERS)] + \
    [_PRE + "Wf", _PRE + "bf"]


def kernel(**inputs):
    import numpy as _np
    import concourse.bacc as _bacc
    from concourse import mybir as _mybir
    from concourse.bass_utils import run_bass_kernel_spmd as _run

    nc = _bacc.Bacc("TRN2", target_bir_lowering=False, num_devices=1)
    arrays, aps = {}, {}
    for name in _INS:
        a = _np.ascontiguousarray(inputs[name])
        arrays[f"in_{name}"] = a
        aps[name] = nc.dram_tensor(f"in_{name}", a.shape, _mybir.dt.from_np(a.dtype), kind="ExternalInput").ap()
    out = nc.dram_tensor("out_y", (B, 1), _mybir.dt.float32, kind="ExternalOutput").ap()
    per_layer = [[aps[_PRE + n + str(l)] for l in range(LAYERS)] for n in ("Wq", "Wk", "Wv", "Wr", "lnw", "lnb")]
    build(nc, aps["r_x"], *per_layer, aps[_PRE + "Wf"], aps[_PRE + "bf"], out)
    r = _run(nc, [arrays], core_ids=[0])
    return r.results[0]["out_y"]
```

```python
import concourse.bass as bass
from concourse import mybir
from contextlib import ExitStack

B, F, E0, D, H, HD, LAYERS = 512, 40, 64, 128, 2, 64, 3
Q, K, V, R = range(4)
SPT = 3
P = SPT * F
TILES = 4
SPG = SPT * TILES
TOK = TILES * P
TH = TILES * H
STREAMS = 4
BODY = STREAMS * LAYERS
FULL = B // (SPG * STREAMS)
PASSES = FULL + 1
UNITS = PASSES * BODY
REST = B - FULL * SPG * STREAMS
REST_TILES = -(-REST // SPT)
LAST_TILES = [(REST_TILES + STREAMS - 1 - s) // STREAMS for s in range(STREAMS)]
LAST_START = B - REST_TILES * SPT
assert 0 < LAST_TILES[-1] <= LAST_TILES[0] < TILES
FULL_ROWS = FULL * STREAMS * TILES
ROWS = FULL_ROWS + REST_TILES
LOT = -(-ROWS // 2)
LOTS = (0, ROWS - LOT)
QPAD = P - F
EPS = 1e-5
W_SCALE = 64.0
SCALE = 1.0 / HD ** 0.5 / W_SCALE ** 2


def build(nc, x, w0, w12, ln, wf_rows_in, lnw_last, lnb_last, bf, out):
    f32 = mybir.dt.float32
    f16 = mybir.dt.float16
    ALU = mybir.AluOpType
    ACT = mybir.ActivationFunctionType
    AX = mybir.AxisListType

    ctx = ExitStack()
    with ctx:
        def sb(name, shape, dt=f32):
            return ctx.enter_context(nc.sbuf_tensor(name, shape, dt))

        def pb(name):
            return ctx.enter_context(nc.psum_tensor(name, [128, 512], f32))

        def sem(name):
            return ctx.enter_context(nc.semaphore(name))

        ident = sb("ident", [128, 128])
        in_sample = sb("in_sample", [P, SPT])
        ones = sb("ones", [128, 128])
        minus_half = sb("minus_half", [P, TILES])
        w_in = sb("w_in", [D, LAYERS, 4, D])
        w_ln = sb("w_ln", [D, LAYERS, 4, D])
        w_hi = sb("w_hi", [D, LAYERS, 4, D], f16)
        w_lo = sb("w_lo", [D, LAYERS, 4, D], f16)
        w0_both = sb("w0_both", [2 * E0, 4, D], f16)
        ln_in = sb("ln_in", [D, 2, LAYERS - 1])
        ln_scaled = sb("ln_scaled", [D, 2, LAYERS - 1])
        lnb_cols = sb("lnb_cols", [D, LAYERS - 1, P])
        qk_bias = sb("qk_bias", [D, LAYERS, 2])
        v_bias = sb("v_bias", [P, LAYERS - 1, D])
        wf_rows = sb("wf_rows", [P, D])
        lnw_rows = sb("lnw_rows", [P, D])
        wf_scaled = sb("wf_scaled", [P, D])
        lnb_rows = sb("lnb_rows", [F, D])
        wfb = sb("wfb", [F, D])
        wfb_sum = sb("wfb_sum", [F, 1])
        bf_col = sb("bf_col", [128, 1])
        neg_bf = sb("neg_bf", [128, 1])

        x_in = sb("x_in", [P, STREAMS, TILES, 2, E0])
        xt_hi = sb("xt_hi", [D, STREAMS, TOK], f16)
        xt_lo = sb("xt_lo", [D, STREAMS, TOK], f16)
        q_hi = sb("q_hi", [D, QPAD + SPG * P], f16)
        q_lo = sb("q_lo", [D, QPAD + SPG * P], f16)
        k_hi = sb("k_hi", [D, SPG, H, F], f16)
        k_lo = sb("k_lo", [D, SPG, H, F], f16)
        v_sb = sb("v_sb", [P, STREAMS, TILES, D])
        smax = sb("smax", [P, TH])
        shifted = sb("shifted", [P, TH, F])
        expd = sb("expd", [P, TH, F])
        ssum = sb("ssum", [P, TH])
        rsum = sb("rsum", [P, TH])
        rsum_own = sb("rsum_own", [P, TH, SPT])
        probs = sb("probs", [P, TH, SPT, F])
        probs_t = sb("probs_t", [P, TH, P])
        o_sb = sb("o_sb", [P, 2, TILES, D])
        stats = sb("stats", [P, 2, TILES, 6])
        mean_var = sb("mean_var", [P, 2, TILES, 2])
        neg_mean = sb("neg_mean", [P, TILES])
        var_eps = sb("var_eps", [P, TILES])
        rstd = sb("rstd", [P, TILES])
        normed = sb("normed", [P, STREAMS, TILES, D])
        weighed = sb("weighed", [P, STREAMS, TILES, D])
        z = sb("z", [P, ROWS])
        e_y = sb("e_y", [LOT, 2, SPT])
        d_y = sb("d_y", [LOT, 2, SPT])
        y = sb("y", [LOT, 2, SPT])

        q_ps, k_ps, v_ps, s_ps, pta_ps, ptb_ps, o_ps, xt_ps = (
            pb(n) for n in ("q_ps", "k_ps", "v_ps", "s_ps", "pta_ps", "ptb_ps", "o_ps", "xt_ps"))
        pt_ps = (pta_ps, ptb_ps)
        bias_ps = s_ps

        w_loaded = [sem("w0_loaded"), sem("w12_loaded")]
        ln_loaded = sem("ln_loaded")
        read_out_loaded = sem("read_out_loaded")
        masks_zeroed = sem("masks_zeroed")
        masks_built = sem("masks_built")
        pads_zeroed = sem("pads_zeroed")
        ln_step = sem("ln_step")
        w0_step = sem("w0_step")
        w_scaled = sem("w_scaled")
        w_hi_done = sem("w_hi_done")
        w_lo_done = sem("w_lo_done")
        w0_both_done = sem("w0_both_done")
        bias_zeroed = sem("bias_zeroed")
        biases_ready = sem("biases_ready")
        biases_copied = sem("biases_copied")
        wf_step = sem("wf_step")
        x_loaded = [sem(f"x{s}_loaded") for s in range(STREAMS)]
        xt_ready = sem("xt_ready")
        xt_hi_copied = sem("xt_hi_copied")
        xt_lo_copied = sem("xt_lo_copied")
        q_ready = sem("q_ready")
        k_ready = sem("k_ready")
        v_ready = sem("v_ready")
        q_hi_copied = sem("q_hi_copied")
        q_lo_copied = sem("q_lo_copied")
        k_hi_copied = sem("k_hi_copied")
        k_lo_copied = sem("k_lo_copied")
        v_copied = sem("v_copied")
        scores_ready = sem("scores_ready")
        max_done = sem("max_done")
        shift_done = sem("shift_done")
        exp_done = sem("exp_done")
        sum_done = sem("sum_done")
        rsum_done = sem("rsum_done")
        rsum_own_done = sem("rsum_own_done")
        probs_done = [sem("probs_a_done"), sem("probs_b_done")]
        pt_ready = [sem("pta_ready"), sem("ptb_ready")]
        pt_copied = [sem("pta_copied"), sem("ptb_copied")]
        o_ready = sem("o_ready")
        relu_done = sem("relu_done")
        stats_done = sem("stats_done")
        mean_var_done = sem("mean_var_done")
        neg_mean_done = sem("neg_mean_done")
        var_eps_done = sem("var_eps_done")
        rstd_done = sem("rstd_done")
        normed_done = sem("normed_done")
        weighed_done = sem("weighed_done")
        z_done = sem("z_done")
        logits_ready = sem("logits_ready")
        y_exp = sem("y_exp")
        head_step = sem("head_step")
        y_ready = sem("y_ready")
        y_written = sem("y_written")
        waits_apart = {e.engine: sem(f"waits_apart_{n}")
                       for n, e in (("pool", nc.gpsimd), ("dve", nc.vector), ("pe", nc.tensor))}

        block = ctx.enter_context(nc.Block())

        def unit(i, j):
            return i * BODY + j

        def layer(j):
            return (j % BODY) // STREAMS

        def in_rows(j):
            return slice(0, E0 if layer(j) == 0 else D)

        def by(i, j, n):
            return i + (j + n) // BODY, (j + n) % BODY

        def exists(i, j):
            return not isinstance(i, int) or 0 <= unit(i, j) < UNITS

        def is_last(i, j):
            return isinstance(i, int) and unit(i, j) == UNITS - 1

        def tiles(i, j):
            return LAST_TILES[j % STREAMS] if isinstance(i, int) and i == FULL else TILES

        def over_slots(engine, slot):
            for j in range(BODY):
                slot(0, j)
            with engine.Fori(1, FULL) as i:
                for j in range(BODY):
                    slot(i, j)
            for j in range(BODY):
                slot(FULL, j)
            for j in range(4):
                slot(PASSES, j)

        def wait_apart(engine, semaphore, count):
            engine.wait_ge(semaphore, count)
            if not isinstance(count, int):
                engine.sem_inc(waits_apart[engine.engine], 1)

        def normalise(engine, half, nt):
            own = slice(half * nt, (half + 1) * nt)
            engine.tensor_tensor(probs[:, own, :, :],
                                 expd[:, own, :].rearrange("p a (s f) -> p a s f", s=1).to_broadcast([P, nt, SPT, F]),
                                 rsum_own[:, own, :].rearrange("p a (s f) -> p a s f", f=1).to_broadcast([P, nt, SPT, F]),
                                 ALU.mult).then_inc(probs_done[half], 1)

        def apply_norm(engine, i, j):
            k = unit(i, j)
            engine.wait_ge(neg_mean_done, k + 1)
            wait_apart(engine, rstd_done, k + 1)
            for t in range(tiles(i, j)):
                ins = engine.tensor_scalar(normed[:, j % STREAMS, t, :], o_sb[:, j % 2, t, :], neg_mean[:, t:t + 1],
                                           rstd[:, t:t + 1], ALU.add, ALU.mult)
            ins.then_inc(normed_done, 1)

        def weigh(engine, i, j):
            nt = tiles(i, j)
            engine.wait_ge(normed_done, unit(i, j) + 1)
            engine.tensor_tensor(weighed[:, j % STREAMS, 0:nt, :], normed[:, j % STREAMS, 0:nt, :],
                                 wf_scaled[:].rearrange("p (a d) -> p a d", a=1).to_broadcast([P, nt, D]),
                                 ALU.mult).then_inc(weighed_done, 1)

        @block.sync
        def _(sp):
            def load_x(stream, start, nt):
                for copy in range(2):
                    sp.dma_start(x_in[:, stream, 0:nt, copy, :],
                                 x[bass.ds(start, nt * SPT)].rearrange("(t s) f e -> (s f) t e", t=nt))\
                        .then_inc(x_loaded[stream], 16)

            load_x(0, 0, TILES)
            sp.dma_start(ln_in[:].rearrange("p a b -> p (a b)"), ln).then_inc(ln_loaded, 16)
            sp.dma_start(w_in[:, 1:, :, :].rearrange("p l n d -> p (l n d)"), w12).then_inc(w_loaded[1], 16)
            load_x(1, SPG, TILES)
            sp.dma_start(wf_rows[:], wf_rows_in).then_inc(read_out_loaded, 16)
            sp.dma_start(lnw_rows[:], lnw_last.rearrange("(a d) -> a d", a=1).to_broadcast([P, D])).then_inc(read_out_loaded, 16)
            sp.dma_start(lnb_rows[:], lnb_last.rearrange("(a d) -> a d", a=1).to_broadcast([F, D])).then_inc(read_out_loaded, 16)
            sp.dma_start(bf_col[:], bf.rearrange("(a d) -> a d", a=1).to_broadcast([128, 1])).then_inc(read_out_loaded, 16)
            for s in range(2, STREAMS):
                load_x(s, s * SPG, TILES)
            with sp.Fori(1, FULL) as i:
                for s in range(STREAMS):
                    sp.wait_ge(xt_ready, unit(i, s) - BODY + 1)
                    load_x(s, i * (STREAMS * SPG) + s * SPG, TILES)
            for s in range(STREAMS):
                sp.wait_ge(xt_ready, unit(FULL - 1, s) + 1)
                load_x(s, LAST_START + sum(LAST_TILES[:s]) * SPT, LAST_TILES[s])

            def store(r0, r1, start, skip=0):
                lot = r0 // LOT
                sp.dma_start(out[start + skip:start + (r1 - r0) * SPT, 0].rearrange("(r s) -> r s", r=r1 - r0),
                             y[r0 - LOTS[lot]:r1 - LOTS[lot], lot, skip:]).then_inc(y_written, 16)

            sp.wait_ge(y_ready, 1)
            store(0, LOT, 0)
            store(LOT, FULL_ROWS, LOT * SPT)
            old = FULL_ROWS * SPT - LAST_START
            row, start = FULL_ROWS + old // SPT, LAST_START + old // SPT * SPT
            store(row, row + 1, start, old % SPT)
            store(row + 1, ROWS, start + SPT)
            sp.wait_ge(y_written, 16 * 4)

        @block.gpsimd
        def _(pool):
            for m in (ident, in_sample):
                pool.memset(m[:], 0.0 if m is ident else 1.0).then_inc(masks_zeroed, 1)
            pool.memset(ones[:], 1.0).then_inc(masks_built, 1)
            pool.memset(minus_half[:], -0.5).then_inc(masks_built, 1)
            pool.wait_ge(masks_zeroed, 2)
            pool.affine_select(out=ident[:], in_=ident[:], compare_op=ALU.not_equal, fill=1.0, base=0,
                               pattern=[[-1, 128]], channel_multiplier=1).then_inc(masks_built, 1)
            pool.affine_select(out=in_sample[:], in_=in_sample[:], compare_op=ALU.is_ge, fill=0.0, base=0,
                               pattern=[[-F, SPT]], channel_multiplier=1).then_inc(masks_zeroed, 1)
            pool.wait_ge(masks_zeroed, 3)
            pool.affine_select(out=in_sample[:], in_=in_sample[:], compare_op=ALU.is_ge, fill=0.0, base=F - 1,
                               pattern=[[F, SPT]], channel_multiplier=-1).then_inc(masks_built, 1)
            for k_part in (k_hi, k_lo):
                pool.memset(k_part[:], 0.0).then_inc(pads_zeroed, 1)
            pool.wait_ge(ln_loaded, 16)
            pool.tensor_scalar(ln_scaled[:], ln_in[:], W_SCALE, None, ALU.mult).then_inc(ln_step, 1)
            pool.wait_ge(ln_step, 1)
            for l in range(LAYERS - 1):
                pool.tensor_scalar(lnb_cols[:, l, :], ones[:, 0:P], ln_scaled[:, 1, l:l + 1], None, ALU.mult).then_inc(ln_step, 1)
            pool.wait_ge(w_loaded[1], 16)
            for l in range(1, LAYERS):
                of_in, of_ln, of_hi, of_lo = (w[:, l, :, :].rearrange("p n d -> p (n d)") for w in (w_in, w_ln, w_hi, w_lo))
                pool.tensor_scalar(of_ln, of_in, ln_scaled[:, 0, l - 1:l], None, ALU.mult).then_inc(w_scaled, 1)
                pool.wait_ge(w_hi_done, l)
                pool.tensor_tensor(of_lo, of_ln, of_hi, ALU.subtract).then_inc(w_lo_done, 1)
            pool.wait_ge(read_out_loaded, 16 * 4)
            pool.tensor_tensor(wf_scaled[:], wf_rows[:], lnw_rows[:], ALU.mult).then_inc(wf_step, 1)
            pool.tensor_tensor(wfb[:], wf_rows[0:F, :], lnb_rows[:], ALU.mult).then_inc(wf_step, 1)
            pool.wait_ge(wf_step, 2)

            def own_inverses(i, j):
                k, th = unit(i, j), tiles(i, j) * H
                pool.wait_ge(rsum_done, k + 1)
                pool.tensor_tensor(rsum_own[:, 0:th, :],
                                   rsum[:, 0:th].rearrange("p (a b) -> p a b", b=1).to_broadcast([P, th, SPT]),
                                   in_sample[:].rearrange("p (a b) -> p a b", a=1).to_broadcast([P, th, SPT]),
                                   ALU.mult).then_inc(rsum_own_done, 1)

            def norm_factors(i, j):
                k, nt = unit(i, j), tiles(i, j)
                if exists(*by(i, j, -1)):
                    wait_apart(pool, normed_done, k)
                wait_apart(pool, mean_var_done, k + 1)
                pool.tensor_scalar(var_eps[:, 0:nt], mean_var[:, j % 2, 0:nt, 1], EPS * W_SCALE ** 2, None, ALU.add)\
                    .then_inc(var_eps_done, 1)
                pool.tensor_scalar(neg_mean[:, 0:nt], mean_var[:, j % 2, 0:nt, 0], -1.0, None, ALU.mult).then_inc(neg_mean_done, 1)
                pool.wait_ge(var_eps_done, k + 1)
                pool.tensor_tensor(rstd[:, 0:nt], var_eps[:, 0:nt], minus_half[:, 0:nt], ALU.pow).then_inc(rstd_done, 1)

            def slot(i, j):
                one, two, three = (by(i, j, -n) for n in (1, 2, 3))
                if exists(*one):
                    own_inverses(*one)
                    pool.wait_ge(rsum_own_done, unit(*one) + 1)
                    normalise(pool, 1, tiles(*one))
                if exists(*three) and layer(three[1]) == LAYERS - 1 and not is_last(*three):
                    weigh(pool, *three)
                if exists(*two):
                    norm_factors(*two)
                    if not is_last(*two):
                        apply_norm(pool, *two)

            over_slots(pool, slot)

        @block.scalar
        def _(act):
            for half in range(2):
                act.dma_start(w_in[half * E0:(half + 1) * E0, 0, :, :].rearrange("p n d -> p (n d)"), w0).then_inc(w_loaded[0], 16)

            def copy_xt_hi(i, j):
                cols = tiles(i, j) * P
                act.wait_ge(xt_ready, unit(i, j) + 1)
                act.activation(xt_hi[:, j % STREAMS, 0:cols], xt_ps[:, 0:cols], ACT.Copy).then_inc(xt_hi_copied, 1)

            copy_xt_hi(0, 0)
            act.wait_ge(pads_zeroed, 4)
            act.wait_ge(bias_zeroed, 1)

            def weights_hi():
                for l in range(1, LAYERS):
                    act.wait_ge(w_scaled, l)
                    act.activation(w_hi[:, l, :, :], w_ln[:, l, :, :], ACT.Copy).then_inc(w_hi_done, 1)

            def copy_biases():
                act.wait_ge(biases_ready, 1)
                rows = (LAYERS - 1) * D
                act.activation(v_bias[:], bias_ps[0:P, 0:rows].rearrange("p (l d) -> p l d", d=D), ACT.Copy)\
                    .then_inc(biases_copied, 1)
                act.activation(qk_bias[:, 1:, :], bias_ps[:, rows:rows + 2 * (LAYERS - 1)].rearrange("p (l n) -> p l n", n=2),
                               ACT.Copy).then_inc(biases_copied, 1)

            def copy_q_hi(i, j):
                k, n = unit(i, j), tiles(i, j) * SPT
                act.wait_ge(q_ready, k + 1)
                act.activation(q_hi[:, QPAD:].rearrange("p (n w) -> p n w", w=P)[:, 0:n, 0:F],
                               q_ps[:, 0:n * F].rearrange("p (n f) -> p n f", f=F), ACT.Identity,
                               bias=qk_bias[:, layer(j), Q:Q + 1]).then_inc(q_hi_copied, 1)

            def copy_k_hi(i, j):
                k, n = unit(i, j), tiles(i, j) * SPT
                act.wait_ge(k_ready, k + 1)
                for h in range(H):
                    rows = slice(h * HD, (h + 1) * HD)
                    act.activation(k_hi[rows, 0:n, h, :], k_ps[rows, 0:n * F].rearrange("p (n f) -> p n f", f=F),
                                   ACT.Identity, bias=qk_bias[rows, layer(j), K:K + 1]).then_inc(k_hi_copied, 1)

            def copy_first_v(i, j):
                k, nt = unit(i, j), tiles(i, j)
                act.wait_ge(v_ready, k + 1)
                act.activation(v_sb[:, j % STREAMS, 0:nt, :], v_ps[0:P, 0:nt * D].rearrange("p (t d) -> p t d", d=D), ACT.Copy)\
                    .then_inc(v_copied, 1)

            def exp(i, j):
                k, th = unit(i, j), tiles(i, j) * H
                act.wait_ge(shift_done, k + 1)
                act.activation(expd[:, 0:th, :], shifted[:, 0:th, :], ACT.Exp, scale=SCALE).then_inc(exp_done, 1)

            def copy_pt(i, j):
                nt = tiles(i, j)
                for half in range(2):
                    act.wait_ge(pt_ready[half], unit(i, j) + 1)
                    act.activation(probs_t[:, half * nt:(half + 1) * nt, :],
                                   pt_ps[half][0:P, 0:nt * P].rearrange("p (a f) -> p a f", f=P), ACT.Copy)\
                        .then_inc(pt_copied[half], 1)

            def relu(i, j):
                k, nt = unit(i, j), tiles(i, j)
                act.wait_ge(o_ready, k + 1)
                if exists(*by(i, j, -2)):
                    act.wait_ge(normed_done, k - 1)
                act.activation(o_sb[:, j % 2, 0:nt, :], o_ps[0:P, 0:nt * D].rearrange("p (t d) -> p t d", d=D), ACT.Relu)\
                    .then_inc(relu_done, 1)

            def read_out(i, j):
                nt, stream = tiles(i, j), j % STREAMS
                group = i * STREAMS + stream
                column = FULL_ROWS + sum(LAST_TILES[:stream]) if isinstance(i, int) and i == FULL else group * TILES
                act.wait_ge(weighed_done, group + 1)
                for t in range(nt):
                    ins = act.activation(weighed[:, stream, t, :], weighed[:, stream, t, :], ACT.Copy,
                                         accum_out=z[:, bass.ds(column + t, 1)])
                ins.then_inc(z_done, 1)

            def slot(i, j):
                now, after, one, two, four = (by(i, j, n) for n in (0, 1, -1, -2, -4))
                if isinstance(i, int) and i == 0 and layer(j) == 1:
                    act.wait_ge(biases_copied, 2)
                if exists(*four) and layer(four[1]) == LAYERS - 1:
                    read_out(*four)
                if exists(*now):
                    copy_q_hi(*now)
                if exists(*one):
                    exp(*one)
                if exists(*now):
                    copy_k_hi(*now)
                if exists(*two):
                    relu(*two)
                if exists(*after):
                    copy_xt_hi(*after)
                if exists(*now) and layer(j) == 0:
                    copy_first_v(*now)
                if isinstance(i, int) and i == 0 and j == 0:
                    weights_hi()
                if isinstance(i, int) and i == 0 and j == 1:
                    copy_biases()
                if exists(*one):
                    copy_pt(*one)

            over_slots(act, slot)
            act.wait_ge(logits_ready, 1)
            act.activation(e_y[:], s_ps[0:LOT, 0:2 * SPT].rearrange("p (a s) -> p a s", a=2), ACT.Exp,
                           scale=-1.0, bias=neg_bf[0:LOT, :]).then_inc(y_exp, 1)

        @block.vector
        def _(dve):
            for q_part in (q_hi, q_lo):
                dve.memset(q_part[:], 0.0).then_inc(pads_zeroed, 1)
            dve.memset(qk_bias[:, 0, :], 0.0).then_inc(bias_zeroed, 1)

            def copy_xt_lo(i, j):
                cols = tiles(i, j) * P
                dve.wait_ge(xt_hi_copied, unit(i, j) + 1)
                dve.tensor_tensor(xt_lo[in_rows(j), j % STREAMS, 0:cols], xt_ps[in_rows(j), 0:cols],
                                  xt_hi[in_rows(j), j % STREAMS, 0:cols], ALU.subtract).then_inc(xt_lo_copied, 1)

            dve.wait_ge(w_loaded[0], 32)
            dve.tensor_scalar(w_ln[:, 0, :, :], w_in[:, 0, :, :], W_SCALE, None, ALU.mult).then_inc(w0_step, 1)
            dve.wait_ge(w0_step, 1)
            dve.tensor_copy(w_hi[:, 0, :, :], w_ln[:, 0, :, :]).then_inc(w0_step, 1)
            dve.wait_ge(w0_step, 2)
            dve.tensor_copy(w0_both[0:E0, :, :], w_hi[0:E0, 0, :, :]).then_inc(w0_both_done, 1)
            dve.tensor_tensor(w0_both[E0:, :, :], w_ln[E0:, 0, :, :], w_hi[E0:, 0, :, :], ALU.subtract)\
                .then_inc(w0_both_done, 1)
            copy_xt_lo(0, 0)

            def copy_q_lo(i, j):
                k, n = unit(i, j), tiles(i, j) * SPT
                dve.wait_ge(q_hi_copied, k + 1)
                hi, lo = (q[:, QPAD:].rearrange("p (n w) -> p n w", w=P)[:, 0:n, 0:F] for q in (q_hi, q_lo))
                dve.scalar_tensor_tensor(lo, q_ps[:, 0:n * F].rearrange("p (n f) -> p n f", f=F),
                                         qk_bias[:, layer(j), Q:Q + 1], hi, ALU.add, ALU.subtract).then_inc(q_lo_copied, 1)

            def copy_k_lo(i, j, h):
                k, n = unit(i, j), tiles(i, j) * SPT
                rows = slice(h * HD, (h + 1) * HD)
                dve.wait_ge(k_hi_copied, 2 * k + h + 1)
                dve.scalar_tensor_tensor(k_lo[rows, 0:n, h, :], k_ps[rows, 0:n * F].rearrange("p (n f) -> p n f", f=F),
                                         qk_bias[rows, layer(j), K:K + 1], k_hi[rows, 0:n, h, :],
                                         ALU.add, ALU.subtract).then_inc(k_lo_copied, 1)

            def copy_v(i, j):
                k, nt = unit(i, j), tiles(i, j)
                dve.wait_ge(v_ready, k + 1)
                dve.tensor_tensor(v_sb[:, j % STREAMS, 0:nt, :], v_ps[0:P, 0:nt * D].rearrange("p (t d) -> p t d", d=D),
                                  v_bias[:, layer(j) - 1:layer(j), :].to_broadcast([P, nt, D]), ALU.add)\
                    .then_inc(v_copied, 1)

            def shift(i, j):
                k, th = unit(i, j), tiles(i, j) * H
                scores = s_ps[0:P, 0:th * F].rearrange("p (a f) -> p a f", f=F)
                dve.wait_ge(scores_ready, k + 1)
                dve.tensor_reduce(smax[:, 0:th], scores, AX.X, ALU.max).then_inc(max_done, 1)
                dve.wait_ge(max_done, k + 1)
                dve.tensor_tensor(shifted[:, 0:th, :], scores,
                                  smax[:, 0:th].rearrange("p (a b) -> p a b", b=1).to_broadcast([P, th, F]),
                                  ALU.subtract).then_inc(shift_done, 1)

            def sum_exps(i, j):
                k, th = unit(i, j), tiles(i, j) * H
                dve.wait_ge(exp_done, k + 1)
                dve.tensor_reduce(ssum[:, 0:th], expd[:, 0:th, :], AX.X, ALU.add).then_inc(sum_done, 1)

            def invert_sums(i, j):
                k, th = unit(i, j), tiles(i, j) * H
                dve.wait_ge(sum_done, k + 1)
                dve.reciprocal(rsum[:, 0:th], ssum[:, 0:th]).then_inc(rsum_done, 1)

            def statistics(i, j):
                k, nt = unit(i, j), tiles(i, j)
                dve.wait_ge(relu_done, k + 1)
                for t in range(nt):
                    ins = dve.bn_stats(stats[:, j % 2, t, :], o_sb[:, j % 2, t, :])
                ins.then_inc(stats_done, 1)

            def moments(i, j):
                k, nt = unit(i, j), tiles(i, j)
                wait_apart(dve, stats_done, k + 1)
                for t in range(nt):
                    ins = dve.bn_aggr(mean_var[:, j % 2, t, :], stats[:, j % 2, t, :])
                ins.then_inc(mean_var_done, 1)

            def slot(i, j):
                now, after, one, two = (by(i, j, n) for n in (0, 1, -1, -2))
                if isinstance(i, int) and i == 0 and layer(j) == 1:
                    dve.wait_ge(biases_copied, 2)
                if exists(*one):
                    shift(*one)
                if exists(*now):
                    copy_q_lo(*now)
                if exists(*one):
                    sum_exps(*one)
                    invert_sums(*one)
                if exists(*now):
                    copy_k_lo(*now, 0)
                if exists(*one):
                    dve.wait_ge(rsum_own_done, unit(*one) + 1)
                    normalise(dve, 0, tiles(*one))
                if exists(*now):
                    copy_k_lo(*now, 1)
                if exists(*two):
                    statistics(*two)
                if exists(*after):
                    copy_xt_lo(*after)
                if exists(*two):
                    moments(*two)
                if exists(*now) and layer(j) > 0:
                    copy_v(*now)
                if is_last(*two):
                    apply_norm(dve, *two)
                    weigh(dve, *two)
                if isinstance(i, int) and i == 0 and j == 1:
                    dve.wait_ge(wf_step, 2)
                    dve.tensor_reduce(wfb_sum[:], wfb[:], AX.X, ALU.add).then_inc(wf_step, 1)
                    dve.tensor_scalar(neg_bf[:], bf_col[:], -1.0, None, ALU.mult).then_inc(wf_step, 1)

            dve.wait_ge(masks_built, 4)
            over_slots(dve, slot)
            dve.wait_ge(y_exp, 1)
            dve.tensor_scalar(d_y[:], e_y[:], 1.0, None, ALU.add).then_inc(head_step, 1)
            dve.wait_ge(head_step, 1)
            dve.reciprocal(y[:], d_y[:]).then_inc(y_ready, 1)

        @block.tensor
        def _(pe):
            def transpose_x(i, j):
                nt, stream = tiles(i, j), j % STREAMS
                wait_apart(pe, x_loaded[stream], i * 32 + 32)
                for t in range(nt):
                    ins = pe.transpose(xt_ps[:, t * P:(t + 1) * P], x_in[:, stream, t, :, :].rearrange("p a e -> p (a e)"),
                                       ident[0:P, 0:P])
                ins.then_inc(xt_ready, 1)

            def transpose_input(i, j):
                if layer(j) == 0:
                    transpose_x(i, j)
                else:
                    pe.wait_ge(normed_done, unit(i, j) - STREAMS + 1)
                    for t in range(tiles(i, j)):
                        ins = pe.transpose(xt_ps[:, t * P:(t + 1) * P], normed[:, j % STREAMS, t, :], ident[0:P, 0:P])
                    ins.then_inc(xt_ready, 1)

            def biases():
                rows = (LAYERS - 1) * D
                pe.wait_ge(w_loaded[1], 16)
                pe.wait_ge(ln_step, LAYERS)
                pe.wait_ge(shift_done, 1)
                for l in range(1, LAYERS):
                    for n in (V, R):
                        pe.matmul(bias_ps[0:P, (l - 1) * D:l * D], lnb_cols[:, l - 1, :], w_in[:, l, n, :],
                                  start=(n == V), stop=(n == R))
                for l in range(1, LAYERS):
                    for n in (Q, K):
                        c = rows + 2 * (l - 1) + n
                        ins = pe.matmul(bias_ps[:, c:c + 1], w_in[:, l, n, :], ln_scaled[:, 1, l - 1:l], start=True, stop=True)
                ins.then_inc(biases_ready, 1)

            def passes(i, j, n, cols):
                x_hi, x_lo = (x[:, j % STREAMS, cols] for x in (xt_hi, xt_lo))
                if layer(j) == 0:
                    return (w0_both[:, n, :], x_hi), (w_hi[0:E0, 0, n, :], x_lo[0:E0])
                hi, lo = (w[:, layer(j), n, :] for w in (w_hi, w_lo))
                return (hi, x_hi), (lo, x_hi), (hi, x_lo)

            def project_features(i, j):
                k, cols = unit(i, j), tiles(i, j) * P
                if isinstance(i, int) and i == 0 and j == 0:
                    pe.wait_ge(w0_both_done, 2)
                elif isinstance(i, int) and i == 0 and j % STREAMS == 0:
                    pe.wait_ge(w_lo_done, layer(j))
                pe.wait_ge(xt_hi_copied, k + 1)
                for n, bank, ready in ((Q, q_ps, q_ready), (K, k_ps, k_ready)):
                    parts = passes(i, j, n, slice(0, cols))
                    for m, (w, xt) in enumerate(parts):
                        if n == Q and m == len(parts) - 1:
                            pe.wait_ge(xt_lo_copied, k + 1)
                        ins = pe.matmul(bank[:, 0:cols], w, xt, start=(m == 0), stop=(m == len(parts) - 1))
                    ins.then_inc(ready, 1)

            def project_tokens(i, j, n, bank, last_stop):
                for t in range(tiles(i, j)):
                    parts = passes(i, j, n, slice(t * P, (t + 1) * P))
                    for m, (w, xt) in enumerate(parts):
                        ins = pe.matmul(bank[0:P, t * D:(t + 1) * D], xt, w, start=(t == 0 and m == 0),
                                        stop=(last_stop and m == len(parts) - 1), skip_group_check=True)
                return ins

            def project_v(i, j):
                if exists(*by(i, j, -1)):
                    pe.wait_ge(v_copied, unit(i, j))
                project_tokens(i, j, V, v_ps, True).then_inc(v_ready, 1)

            def project_residual(i, j):
                if exists(*by(i, j, -1)):
                    pe.wait_ge(relu_done, unit(i, j))
                project_tokens(i, j, R, o_ps, False)

            def scores(i, j):
                k = unit(i, j)
                if isinstance(i, int) and i == 0 and j == 1:
                    pe.wait_ge(biases_copied, 2)
                pe.wait_ge(q_hi_copied, k + 1)
                pe.wait_ge(k_hi_copied, 2 * k + 2)
                pe.wait_ge(q_lo_copied, k + 1)
                pe.wait_ge(k_lo_copied, 2 * k + 2)
                for t in range(tiles(i, j)):
                    for s in range(SPT):
                        n = t * SPT + s
                        at = QPAD + n * P - s * F
                        for m, (q, kk) in enumerate(((q_hi, k_hi), (q_hi, k_lo), (q_lo, k_hi))):
                            ins = pe.matmul(s_ps[0:P, t * H * F:(t + 1) * H * F], q[:, at:at + P],
                                            kk[:, n, :, :].rearrange("p h f -> p (h f)"),
                                            start=(s == 0 and m == 0), stop=(s == SPT - 1 and m == 2))
                ins.then_inc(scores_ready, 1)

            def transpose_probs(i, j):
                nt = tiles(i, j)
                for half in range(2):
                    pe.wait_ge(probs_done[half], unit(i, j) + 1)
                    for a in range(nt):
                        ins = pe.transpose(pt_ps[half][0:P, a * P:(a + 1) * P],
                                           probs[:, half * nt + a, :, :].rearrange("p s f -> p (s f)"), ident[0:P, 0:P])
                    ins.then_inc(pt_ready[half], 1)

            def attend(i, j):
                k, nt = unit(i, j), tiles(i, j)
                pe.wait_ge(v_copied, k + 1)
                for a in range(2 * nt):
                    if a % nt == 0:
                        pe.wait_ge(pt_copied[a // nt], k + 1)
                    ins = pe.matmul(o_ps[0:P, a * HD:(a + 1) * HD], probs_t[:, a, :],
                                    v_sb[:, j % STREAMS, a // H, a % H * HD:(a % H + 1) * HD],
                                    start=False, stop=True, skip_group_check=True)
                ins.then_inc(o_ready, 1)

            def slot(i, j):
                now, after, one, two = (by(i, j, n) for n in (0, 1, -1, -2))
                if exists(*now):
                    project_features(*now)
                if exists(*two):
                    attend(*two)
                if exists(*now):
                    project_v(*now)
                if exists(*after):
                    transpose_input(*after)
                if exists(*one):
                    project_residual(*one)
                if exists(*one):
                    if isinstance(i, int) and i == 0 and j == 1:
                        biases()
                    transpose_probs(*one)
                if exists(*now):
                    scores(*now)

            pe.wait_ge(masks_built, 4)
            transpose_input(0, 0)
            over_slots(pe, slot)
            pe.wait_ge(wf_step, 4)
            pe.wait_ge(z_done, PASSES * STREAMS)
            for lot, r0 in enumerate(LOTS):
                to = s_ps[0:LOT, lot * SPT:(lot + 1) * SPT]
                pe.matmul(to, z[:, r0:r0 + LOT], in_sample[:], start=True, stop=False)
                ins = pe.matmul(to, ones[0:F, 0:LOT], wfb_sum[:].to_broadcast([F, SPT]), start=False, stop=True)
            ins.then_inc(logits_ready, 1)


_PRE = "L0_rec_"


def kernel(**inputs):
    import numpy as _np
    import concourse.bacc as _bacc
    from concourse import mybir as _mybir
    from concourse.bass_utils import run_bass_kernel_spmd as _run

    def of(name, l):
        return _np.asarray(inputs[f"{_PRE}{name}{l}"])

    def weights(layers):
        return _np.concatenate([of(n, l).T for l in layers for n in ("Wq", "Wk", "Wv", "Wr")], axis=1)

    last = LAYERS - 1
    wf = _np.asarray(inputs[_PRE + "Wf"]).reshape(F, D)
    arrays = {
        "x": _np.asarray(inputs["r_x"]),
        "w0": weights([0]),
        "w12": weights(range(1, LAYERS)),
        "ln": _np.stack([of(n, l) for n in ("lnw", "lnb") for l in range(last)], axis=1),
        "wf_rows": _np.concatenate([wf] * SPT, axis=0),
        "lnw_last": of("lnw", last),
        "lnb_last": of("lnb", last),
        "bf": _np.asarray(inputs[_PRE + "bf"]),
    }
    nc = _bacc.Bacc("TRN2", target_bir_lowering=False, num_devices=1)
    arrays = {f"in_{n}": _np.ascontiguousarray(a) for n, a in arrays.items()}
    args = [nc.dram_tensor(n, a.shape, _mybir.dt.from_np(a.dtype), kind="ExternalInput").ap() for n, a in arrays.items()]
    out = nc.dram_tensor("out_y", (B, 1), _mybir.dt.float32, kind="ExternalOutput").ap()
    build(nc, *args, out)
    r = _run(nc, [arrays], core_ids=[0])
    return r.results[0]["out_y"]
```
